# Optimizing a Trainium2 kernel written in Bass

```python
import numpy as np
import jax
import jax.numpy as jnp

def _softmax(x, axis=-1):
    return jax.nn.softmax(x, axis=axis)

def _gelu(x):
    return jax.nn.gelu(x, approximate=True)

def _silu(x):
    return jax.nn.silu(x)

def _sigmoid(x):
    return jax.nn.sigmoid(x)

def _layernorm(x, axis=-1, eps=1e-05):
    m = jnp.mean(x, axis=axis, keepdims=True)
    v = jnp.var(x, axis=axis, keepdims=True)
    return (x - m) / jnp.sqrt(v + eps)

def _scatter_add(tgt, idx, src, axis=0):
    return tgt.at[idx].add(src)

def _segment_sum(src, seg, n):
    return jax.ops.segment_sum(src, seg, n)
kernel_name = 'mk_adj_resnorm_d4_adj_r2_b09a2d'

def setup_inputs(seed: int=0):
    np.random.seed(seed)
    _w = jnp.asarray

    def _rec_inputs():
        import jax
        import jax.numpy as jnp
        _gk = jax.random.key(seed)
        x = -0.003407 + 1.001 * jax.random.normal(jax.random.fold_in(_gk, 1), (1354, 128), jnp.float32)
        _a = jax.random.bernoulli(jax.random.fold_in(_gk, 2), 0.0014771, (1354, 1354))
        _a = jnp.logical_or(_a, jnp.swapaxes(_a, -1, -2))
        _a = jnp.logical_or(_a, jnp.eye(1354, dtype=bool))
        _af = _a.astype(jnp.float32)
        _af = _af * jax.random.uniform(jax.random.fold_in(_gk, 3), (1354, 1354), jnp.float32, 0.05, 5.06092)
        adj = _af
        return (x, adj)
    x, adj = _rec_inputs()

    def _L0_gnn_setup():
        import jax, jax.numpy as jnp
        import numpy as np
        N = 512
        D = 128
        H = 8
        key = jax.random.key(seed)
        ks = jax.random.split(key, 7)
        s = (D * H) ** (-0.5)
        return {'x': jax.random.normal(ks[0], (N, D), dtype=jnp.float32), 'spatial_encoding': jax.random.normal(ks[1], (N, N), dtype=jnp.float32), 'edge_encoding': jax.random.normal(ks[2], (N, N), dtype=jnp.float32), 'Wq': jax.random.normal(ks[3], (D * H, D), dtype=jnp.float32) * s, 'Wk': jax.random.normal(ks[4], (D * H, D), dtype=jnp.float32) * s, 'Wv': jax.random.normal(ks[5], (D * H, D), dtype=jnp.float32) * s, 'Wo': jax.random.normal(ks[6], (D, D * H), dtype=jnp.float32) * s}
    _L0_gnn_all = _L0_gnn_setup()
    _L0_gnn_in = {k: v for k, v in _L0_gnn_all.items() if k in ('Wq', 'Wk', 'Wv', 'Wo')}
    del _L0_gnn_all

    def _L1_gnn_setup():
        import jax, jax.numpy as jnp
        import numpy as np
        N = 8192
        U = 128
        AVG_DEGREE = 32
        key = jax.random.key(seed)
        kx, ka, kw = jax.random.split(key, 3)
        x = jax.random.normal(kx, (N, U), dtype=jnp.float32)
        adj = (jax.random.uniform(ka, (N, N)) < AVG_DEGREE / N).astype(jnp.float32)
        W = jax.random.normal(kw, (U, U), dtype=jnp.float32) * 0.05
        b = jnp.zeros((U,), dtype=jnp.float32)
        return {'x': x, 'adj': adj, 'W': W, 'b': b}
    _L1_gnn_all = _L1_gnn_setup()
    _L1_gnn_in = {k: v for k, v in _L1_gnn_all.items() if k in ('W', 'b')}
    del _L1_gnn_all

    def _L2_gnn_setup():
        import jax, jax.numpy as jnp
        import numpy as np
        N, F, UNITS = (8192, 128, 128)
        key = jax.random.key(seed)
        k1, k2, k3 = jax.random.split(key, 3)
        features = jax.random.normal(k1, (N, F), dtype=jnp.float32)
        A = jax.random.uniform(k2, (N, N), dtype=jnp.float32)
        kernel = jax.random.normal(k3, (F, UNITS), dtype=jnp.float32) * (1.0 / np.sqrt(F))
        bias = jnp.zeros((UNITS,), dtype=jnp.float32)
        return {'features': features, 'A': A, 'kernel': kernel, 'bias': bias}
    _L2_gnn_all = _L2_gnn_setup()
    _L2_gnn_in = {k: v for k, v in _L2_gnn_all.items() if k in ('kernel', 'bias')}
    del _L2_gnn_all

    def _L3_gnn_setup():
        import jax, jax.numpy as jnp
        import numpy as np
        NEG_SLOPE = 0.01
        N_U, N_V = (4096, 4096)
        U_F, V_F = (128, 128)
        HIDS = [128, 128]
        NUM_ROUNDS = 3

        def _glorot(key, fan_in, fan_out):
            lim = np.sqrt(6.0 / (fan_in + fan_out)).astype(np.float32)
            return jax.random.uniform(key, (fan_in, fan_out), jnp.float32, -lim, lim)

        def _mlp(x, W1, b1, W2, b2, W3, b3):
            a = jax.nn.leaky_relu
            x = a(x @ W1 + b1, NEG_SLOPE)
            x = a(x @ W2 + b2, NEG_SLOPE)
            return a(x @ W3 + b3, NEG_SLOPE)
        key = jax.random.key(seed)
        ks = jax.random.split(key, 12)
        inp = {'u_node_feats': jax.random.normal(ks[0], (N_U, U_F), jnp.float32), 'v_node_feats': jax.random.normal(ks[1], (N_V, V_F), jnp.float32), 'uv_adj_mat': jax.random.uniform(ks[2], (N_V, N_U), jnp.float32), 'vu_adj_mat': jax.random.uniform(ks[3], (N_U, N_V), jnp.float32)}
        dims_uv = [U_F] + HIDS + [V_F]
        dims_vu = [V_F] + HIDS + [U_F]
        k = 4
        for tag, dims in (('uv', dims_uv), ('vu', dims_vu)):
            for i in range(3):
                inp[f'{tag}_W{i + 1}'] = _glorot(ks[k], dims[i], dims[i + 1])
                k += 1
                inp[f'{tag}_b{i + 1}'] = jnp.zeros((dims[i + 1],), jnp.float32)
        return inp
    _L3_gnn_all = _L3_gnn_setup()
    _L3_gnn_in = {k: v for k, v in _L3_gnn_all.items() if k in ('v_node_feats', 'uv_W1', 'uv_b1', 'uv_W2', 'uv_b2', 'uv_W3', 'uv_b3', 'vu_W1', 'vu_b1', 'vu_W2', 'vu_b2', 'vu_W3', 'vu_b3')}
    del _L3_gnn_all
    return {'x': x, 'adj': adj, 'L0_gnn_Wq': _L0_gnn_in['Wq'], 'L0_gnn_Wk': _L0_gnn_in['Wk'], 'L0_gnn_Wv': _L0_gnn_in['Wv'], 'L0_gnn_Wo': _L0_gnn_in['Wo'], 'L1_gnn_W': _L1_gnn_in['W'], 'L1_gnn_b': _L1_gnn_in['b'], 'L2_gnn_kernel': _L2_gnn_in['kernel'], 'L2_gnn_bias': _L2_gnn_in['bias'], 'L3_gnn_v_node_feats': _L3_gnn_in['v_node_feats'], 'L3_gnn_uv_W1': _L3_gnn_in['uv_W1'], 'L3_gnn_uv_b1': _L3_gnn_in['uv_b1'], 'L3_gnn_uv_W2': _L3_gnn_in['uv_W2'], 'L3_gnn_uv_b2': _L3_gnn_in['uv_b2'], 'L3_gnn_uv_W3': _L3_gnn_in['uv_W3'], 'L3_gnn_uv_b3': _L3_gnn_in['uv_b3'], 'L3_gnn_vu_W1': _L3_gnn_in['vu_W1'], 'L3_gnn_vu_b1': _L3_gnn_in['vu_b1'], 'L3_gnn_vu_W2': _L3_gnn_in['vu_W2'], 'L3_gnn_vu_b2': _L3_gnn_in['vu_b2'], 'L3_gnn_vu_W3': _L3_gnn_in['vu_W3'], 'L3_gnn_vu_b3': _L3_gnn_in['vu_b3']}

def reference(x, adj, L0_gnn_Wq, L0_gnn_Wk, L0_gnn_Wv, L0_gnn_Wo, L1_gnn_W, L1_gnn_b, L2_gnn_kernel, L2_gnn_bias, L3_gnn_v_node_feats, L3_gnn_uv_W1, L3_gnn_uv_b1, L3_gnn_uv_W2, L3_gnn_uv_b2, L3_gnn_uv_W3, L3_gnn_uv_b3, L3_gnn_vu_W1, L3_gnn_vu_b1, L3_gnn_vu_W2, L3_gnn_vu_b2, L3_gnn_vu_W3, L3_gnn_vu_b3):
    import jax
    import jax.numpy as jnp

    def _L0_gnn_ref(x, spatial_encoding, edge_encoding, Wq, Wk, Wv, Wo):
        import jax, jax.numpy as jnp
        import numpy as np
        N = 512
        D = 128
        H = 8
        n, d = x.shape
        h = Wq.shape[0] // d
        scale = d ** (-0.5)
        q = (x @ Wq.T).reshape(d, n, h)
        k = (x @ Wk.T).reshape(d, n, h)
        v = (x @ Wv.T).reshape(d, n, h)
        a = jnp.einsum('dnh,dmh->dnm', q, k) * scale
        a = a + spatial_encoding + edge_encoding
        a = jax.nn.softmax(a, axis=2)
        out = jnp.einsum('dnm,dmh->dnh', a, v)
        out = out.reshape(n, h * d)
        return out @ Wo.T

    def _L1_gnn_ref(x, adj, W, b):
        import jax, jax.numpy as jnp
        import numpy as np
        N = 8192
        U = 128
        AVG_DEGREE = 32
        adj = jax.lax.stop_gradient(adj)
        neigh1 = adj @ x
        x1 = jax.nn.swish(neigh1 @ W + b)
        neigh2 = adj @ x1
        x2 = jax.nn.swish(neigh2 @ W + b)
        return x2

    def _L2_gnn_ref(features, A, kernel, bias):
        import jax, jax.numpy as jnp
        import numpy as np
        N, F, UNITS = (8192, 128, 128)
        agg = jnp.matmul(A, features)
        out = jnp.matmul(agg, kernel) + bias
        return jax.nn.relu(out)

    def _L3_gnn_ref(u_node_feats, v_node_feats, uv_adj_mat, vu_adj_mat, uv_W1, uv_b1, uv_W2, uv_b2, uv_W3, uv_b3, vu_W1, vu_b1, vu_W2, vu_b2, vu_W3, vu_b3):
        import jax, jax.numpy as jnp
        import numpy as np
        NEG_SLOPE = 0.01
        N_U, N_V = (4096, 4096)
        U_F, V_F = (128, 128)
        HIDS = [128, 128]
        NUM_ROUNDS = 3

        def _glorot(key, fan_in, fan_out):
            lim = np.sqrt(6.0 / (fan_in + fan_out)).astype(np.float32)
            return jax.random.uniform(key, (fan_in, fan_out), jnp.float32, -lim, lim)

        def _mlp(x, W1, b1, W2, b2, W3, b3):
            a = jax.nn.leaky_relu
            x = a(x @ W1 + b1, NEG_SLOPE)
            x = a(x @ W2 + b2, NEG_SLOPE)
            return a(x @ W3 + b3, NEG_SLOPE)
        u, v = (u_node_feats, v_node_feats)
        for _ in range(NUM_ROUNDS):
            v = _mlp(uv_adj_mat @ u, uv_W1, uv_b1, uv_W2, uv_b2, uv_W3, uv_b3)
            u = _mlp(vu_adj_mat @ v, vu_W1, vu_b1, vu_W2, vu_b2, vu_W3, vu_b3)
        return v
    x = _layernorm(x + _L0_gnn_ref(x, adj, adj, L0_gnn_Wq, L0_gnn_Wk, L0_gnn_Wv, L0_gnn_Wo), axis=-1)
    x = _layernorm(x + _L1_gnn_ref(x, adj, L1_gnn_W, L1_gnn_b), axis=-1)
    x = _layernorm(x + _L2_gnn_ref(x, adj, L2_gnn_kernel, L2_gnn_bias), axis=-1)
    x = _layernorm(x + _L3_gnn_ref(x, L3_gnn_v_node_feats, adj, adj, L3_gnn_uv_W1, L3_gnn_uv_b1, L3_gnn_uv_W2, L3_gnn_uv_b2, L3_gnn_uv_W3, L3_gnn_uv_b3, L3_gnn_vu_W1, L3_gnn_vu_b1, L3_gnn_vu_W2, L3_gnn_vu_b2, L3_gnn_vu_W3, L3_gnn_vu_b3), axis=-1)
    return x

_drawn_inputs = setup_inputs


def setup_inputs(seed=0):
    import zlib

    import numpy as np

    out = dict(_drawn_inputs(seed))
    spreads = {'L1_gnn_b': (0.0, 0.285),
     'L2_gnn_bias': (0.0, 0.8),
     'L3_gnn_uv_b1': (0.0, 0.8),
     'L3_gnn_uv_b2': (0.0, 0.617),
     'L3_gnn_uv_b3': (0.0, 0.469),
     'L3_gnn_vu_b1': (0.0, 2.0),
     'L3_gnn_vu_b2': (0.0, 2.0),
     'L3_gnn_vu_b3': (0.0, 0.8)}
    factors = {'L0_gnn_Wq': 8.0, 'L0_gnn_Wk': 8.0}
    for name, (base, spread) in spreads.items():
        noise = np.random.default_rng([zlib.crc32(name.encode()), seed]).standard_normal(out[name].shape)
        drawn = base * np.exp(spread * noise) if base else spread * noise
        out[name] = jnp.asarray(drawn.astype(out[name].dtype))
    for name, factor in factors.items():
        out[name] = (out[name] * factor).astype(out[name].dtype)
    return out
```

```python
from contextlib import ExitStack

import concourse.bass as bass
from concourse import mybir

F32 = mybir.dt.float32
BF16 = mybir.dt.bfloat16
ALU = mybir.AluOpType
ACT = mybir.ActivationFunctionType
AX = mybir.AxisListType

N = 1354
D = 128
H = 8
P = 128
T = -(-N // P)
NPAD = T * P
KROWS = -(-N // T)
NKEYS = [KROWS if t < N - T * (KROWS - 1) else KROWS - 1 for t in range(T)]
RP = [min(P, N - P * i) for i in range(T)]
G = N * D
SCALE = float(D) ** -0.5
EPS = 1e-5

HG = 4
NG = D // HG
CW = [452, 452, 450]
C0 = [0, 452, 904]
MW = 452
M0 = [0, 451, 902]
NC = len(CW)
STEPS = NC * T
PAIRS = HG * T * NC // 2
SLOTS = PAIRS + 1
PARTS = 3
SROWS = PARTS * PARTS * H
ZROWS = 96
MAXROWS = ZROWS + PARTS
ALLROWS = MAXROWS + PARTS
V1 = H + 1

RING = 6
LAG = 4
ACT_LEAD = RING
DVE_LEAD = RING
S_FIRST, S_LAST = 2, 30
ADD, MUL = "a", "m"
KIND = "".join(ADD if s in (0, 1, 4, 7, 10, 13, 16, 19, 22, 26, 31, 32) else MUL for s in range(STEPS))
PAIRS_AT = [0] * STEPS
for _s in range(S_FIRST, S_LAST + 1):
    _n = S_LAST + 1 - S_FIRST
    PAIRS_AT[_s] = (_s + 1 - S_FIRST) * PAIRS // _n - (_s - S_FIRST) * PAIRS // _n
PAIR_FROM = [sum(PAIRS_AT[:s]) for s in range(STEPS)]
ADDS = KIND.count(ADD)
MULS = KIND.count(MUL)


def adds_before(u):
    return u // STEPS * ADDS + KIND[: u % STEPS].count(ADD)


def muls_before(u):
    return u // STEPS * MULS + KIND[: u % STEPS].count(MUL)


def kind(u):
    return KIND[u % STEPS]


UV, VU = (2, 3, 4), (5, 6, 7)
PROPS = [("x", (0,), "silu"), ("out", (0,), "silu"), ("x", (1,), "relu"),
         ("x", UV, "leaky"), ("out", VU, "leaky"), ("out", UV, "leaky"), ("out", VU, "leaky"), ("out", UV, "leaky")]
NORM_AFTER = {1: 1, 2: 2, 7: 3}


def wave(layers):
    return [(st, c - st) for c in range(NC + layers) for st in range(layers + 1) if 0 <= c - st < NC]


def build(nc, x, adj, wqkv, wo, weights, biases, out):
    ctx = ExitStack()
    with ctx:
        def sem(name):
            return ctx.enter_context(nc.semaphore(name))

        def sb(name, shape, dt):
            return ctx.enter_context(nc.sbuf_tensor(name, shape, dt))

        qk_parts = nc.dram_tensor("qk_parts", [2, PARTS, H, G], BF16, kind="Internal").ap()
        v_rows = nc.dram_tensor("v_rows", [G * V1], F32, kind="Internal").ap()
        att = nc.dram_tensor("att", [V1, G], F32, kind="Internal").ap()

        adjT = sb("adjT", [P, T, N], F32)
        xT = sb("xT", [P, NPAD], F32)
        woT = sb("woT", [P, H, D], F32)
        wts = sb("wts", [P, 8, D], F32)
        bia = sb("bia", [P, 8], F32)
        ident = sb("ident", [P, P], F32)
        v_sb = sb("v_sb", [P, 2, HG, T * V1], F32)
        o_sb = sb("o_sb", [P, 2, 512], F32)
        maxes = sb("maxes", [P, 2 * PAIRS], F32)
        negmax = sb("negmax", [P, P], F32)
        rowrem = sb("rowrem", [HG * T, P], F32)
        rowparts = sb("rowparts", [HG * T, PARTS, P], BF16)
        biasrow = sb("biasrow", [PARTS, NPAD], BF16)
        ones3 = sb("ones3", [PARTS, KROWS], BF16)
        epst = sb("epst", [P, 1], F32)
        avg = sb("avg", [P, P], F32)

        EBSZ = MULS * 452
        QSZ, KSZ = 2 * HG * NPAD // 2, 2 * HG * N // 2
        RSZ = RING * HG * 452
        arena = sb("arena", [P, EBSZ + QSZ + KSZ + RSZ], F32)
        EB0, Q0, K0, R0 = 0, EBSZ, EBSZ + QSZ, EBSZ + QSZ + KSZ

        def carve(at, shape, rows=P, dt=F32):
            size = 1
            for n in shape:
                size *= n
            words = size if dt == F32 else size // 2
            v = arena[0:rows, at:at + words]
            if dt != F32:
                v = v.bitcast(dt)
            if len(shape) == 1:
                return v
            names = "abcd"[: len(shape)]
            return v.rearrange(f"p ({' '.join(names)}) -> p {' '.join(names)}",
                               **{k: n for k, n in zip(names, shape)})

        ebias = carve(EB0, [MULS, 452])
        q_sb = carve(Q0, [2, HG, NPAD], P, BF16)
        k_sb = carve(K0, [2, HG, N], P, BF16)
        ring = carve(R0, [RING, HG, 452])

        x_nat = carve(EB0, [T, D])
        wT = carve(EB0 + T * D, [3, 1024])
        rem = [carve(EB0 + T * D + 3072 + 1024 * i, [1024]) for i in range(2)]
        assert T * D + 3072 + 2048 <= EBSZ
        w_nat = carve(R0, [4, H, D])
        parts = [carve(R0 + 4096 + 1536 * i, [PARTS, 1024], P, BF16) for i in range(2)]
        v_out = [carve(R0 + 4096 + 3072, [P, V1]), carve(EB0 + T * D + 5120, [P, V1])]
        adj_nat = [carve(R0 + NPAD * i, [NPAD]) for i in range(2)]
        assert 4096 + 3072 + P * V1 <= RSZ and T * D + 5120 + P * V1 <= EBSZ and 2 * NPAD <= 4096

        at = 0
        oT = carve(0, [H, N]); at += H * N
        o_nat = [carve(at + V1 * P * i, [V1, P]) for i in range(3)]; at += 3 * V1 * P
        rsum = [carve(at + P * i, [P]) for i in range(2)]; at += 2 * P
        z_sb = carve(at, [N]); at += N
        mid = [carve(at + N * i, [N]) for i in range(2)]; at += 2 * N
        leak = carve(at, [N]); at += N
        out_sb = carve(at, [NPAD]); at += NPAD
        cen = carve(at, [N]); at += N
        sq = carve(at, [N]); at += N
        nat = carve(at, [T, D]); at += T * D
        assert at <= EBSZ + QSZ + KSZ + RSZ

        ps = ctx.enter_context(nc.psum_tensor("ps", [P, 8, 512], F32))
        ST_BANK, PV_BANK = 4, 7

        s_ident = sem("s_ident")
        w_loaded = sem("w_loaded")
        x_loaded = sem("x_loaded")
        small_loaded = sem("small_loaded")
        fill = sem("fill")
        wt_ready = sem("wt_ready")
        wt_read = sem("wt_read")
        proj_ready = sem("proj_ready")
        proj_read = sem("proj_read")
        rem1_ready = sem("rem1_ready")
        part2_ready = sem("part2_ready")
        part3_ready = sem("part3_ready")
        parts_stored = [sem(f"parts_stored{i}") for i in range(2)]
        v_stored = [sem(f"v_stored{i}") for i in range(2)]
        adj_loaded = [sem(f"adj_loaded{i}") for i in range(2)]
        adjt_ready = sem("adjt_ready")
        adjt_read = sem("adjt_read")
        bmax_ready = sem("bmax_ready")
        brow_ready = sem("brow_ready")
        brow_step = sem("brow_step")
        brow_copied = sem("brow_copied")
        bb_ready = sem("bb_ready")
        eb_sum = sem("eb_sum")
        eb_ready = sem("eb_ready")
        pv_clear = sem("pv_clear")
        qk_loaded = [sem(f"qk_loaded{i}") for i in range(2)]
        v_loaded = [sem(f"v_loaded{i}") for i in range(2)]
        maxrow_loaded = [sem(f"maxrow_loaded{i}") for i in range(2)]
        s_ready = sem("s_ready")
        s_read = sem("s_read")
        negmax_ready = sem("negmax_ready")
        split_step = sem("split_step")
        st_ready = sem("st_ready")
        exps_done = sem("exps_done")
        adds_done = sem("adds_done")
        sbexp_done = sem("sbexp_done")
        mults_done = sem("mults_done")
        pv_done = sem("pv_done")
        o_copied = sem("o_copied")
        o_stored = [sem(f"o_stored{i}") for i in range(2)]
        on_loaded = [sem(f"on_loaded{i}") for i in range(3)]
        rsum_ready = sem("rsum_ready")
        on_ready = sem("on_ready")
        ot_ready = sem("ot_ready")
        ot_read = sem("ot_read")
        y_ready = sem("y_ready")
        z_ready = sem("z_ready")
        mean_ready = sem("mean_ready")
        cen_ready = sem("cen_ready")
        sq_ready = sem("sq_ready")
        var_ready = sem("var_ready")
        std_ready = sem("std_ready")
        inv_ready = sem("inv_ready")
        x_ready = sem("x_ready")
        nat_ready = sem("nat_ready")
        nat_read = sem("nat_read")
        agg_ready = sem("agg_ready")
        agg_read = sem("agg_read")
        dense_ready = sem("dense_ready")
        act_done = sem("act_done")
        leaky_done = sem("leaky_done")
        out_stored = sem("out_stored")

        block = ctx.enter_context(nc.Block())

        N_ADJ = 3
        TB = [(0, 4), (4, 4), (8, T - 8)]

        @block.sync
        def _(sp):
            sp.dma_start(w_nat[:, 0, :, :], wqkv[0].rearrange("(j h) c -> j h c", h=H)).then_inc(w_loaded, 16)
            sp.dma_start(x_nat[:, 0:T - 1, :], x[0:(T - 1) * P, :].rearrange("(i p) d -> p i d", p=P)).then_inc(x_loaded, 16)
            sp.dma_start(x_nat[0:RP[-1], T - 1, :], x[(T - 1) * P:N, :]).then_inc(x_loaded, 16)
            for w in (1, 2):
                sp.dma_start(w_nat[:, w, :, :], wqkv[w].rearrange("(j h) c -> j h c", h=H)).then_inc(w_loaded, 16)
            sp.dma_start(w_nat[:, 3, :, :].rearrange("p h d -> p (h d)"), wo).then_inc(w_loaded, 16)
            for n in range(8):
                sp.dma_start(wts[:, n, :], weights[n]).then_inc(small_loaded, 16)
                sp.dma_start(bia[:, n:n + 1], biases[n].rearrange("(d o) -> d o", o=1)).then_inc(small_loaded, 16)

            def load_adj(i):
                if i == 0:
                    sp.wait_ge(wt_ready, 11)
                if i >= 2:
                    sp.wait_ge(adjt_ready, N_ADJ * (i - 1))
                    sp.wait_ge(bmax_ready, i - 1)
                sp.dma_start(adj_nat[i % 2][0:RP[i], 0:N], adj[P * i:P * i + RP[i], :]).then_inc(adj_loaded[i % 2], 16)

            for i in range(2):
                load_adj(i)
            for i in range(T):
                r = RP[i]
                for w in range(2):
                    e = 2 * i + w
                    sp.wait_ge(part3_ready, e + 1)
                    for k in range(PARTS):
                        sp.dma_start(qk_parts[w, k, :, P * P * i:P * P * i + r * P].rearrange("h (r j) -> r h j", j=P),
                                     parts[e % 2][0:r, k, :].rearrange("p (h j) -> p h j", h=H)).then_inc(parts_stored[e % 2], 16)
                sp.wait_ge(proj_read, 3 * i + 3)
                sp.dma_start(v_rows[P * P * V1 * i:P * V1 * (P * i + r)].rearrange("(r j) -> r j", j=P * V1),
                             v_out[i % 2][0:r, :, :].rearrange("p j h -> p (j h)")).then_inc(v_stored[i % 2], 16)
            for i in range(2):
                sp.wait_ge(parts_stored[i], 48 * T)
                sp.wait_ge(v_stored[i], 16 * len(range(i, T, 2)))

            def load_qk(g, par):
                for b in range(PARTS):
                    sp.dma_start(q_sb[24 * b:24 * b + 24, par, :, 0:N],
                                 qk_parts[0].rearrange("k h g -> (k h) g")[:, bass.ds(g * (HG * N), HG * N)]
                                 .rearrange("r (a n) -> r a n", a=HG)).then_inc(qk_loaded[par], 16)
                    for a in range(PARTS):
                        sp.dma_start(k_sb[24 * b + 8 * a:24 * b + 8 * a + 8, par, :, :].rearrange("r a n -> r (a n)"),
                                     qk_parts[1, b, :, bass.ds(g * (HG * N), HG * N)]).then_inc(qk_loaded[par], 16)

            def load_v(g, par):
                src = v_rows[bass.ds(g * (HG * N * V1), HG * N * V1)].rearrange("(a m) -> a m", a=HG)
                full = (KROWS - 1) * T * V1
                sp.dma_start(v_sb[0:KROWS - 1, par, :, :],
                             src[:, 0:full].rearrange("a (p x) -> p a x", x=T * V1)).then_inc(v_loaded[par], 16)
                sp.dma_start(v_sb[KROWS - 1:KROWS, par, :, 0:V1], src[:, full:full + V1].rearrange("(o a) x -> o a x", o=1)).then_inc(v_loaded[par], 16)

            def maxrows(par):
                for k in range(PARTS):
                    sp.dma_start(q_sb[ZROWS + k:ZROWS + k + 1, par, :, :].rearrange("o a (i j) -> o (a i) j", j=P),
                                 rowparts[:, k, :]).then_inc(maxrow_loaded[par], 16)

            def store(g, q, c, cnt):
                sp.wait_ge(o_copied, cnt + 1)
                for a in range(HG):
                    sp.dma_start(att[:, bass.ds(g * (HG * N) + (a * N + C0[c]), CW[c])],
                                 o_sb[32 * a:32 * a + V1, q % 2, 0:CW[c]]).then_inc(o_stored[q % 2], 16)

            sp.wait_ge(fill, 4)
            load_qk(0, 0)
            load_qk(1, 1)
            load_v(0, 0)
            load_v(1, 1)
            for i in range(2, T):
                load_adj(i)
            sp.wait_ge(brow_step, 4)
            for k in range(PARTS):
                sp.dma_start(biasrow[k:k + 1, :].rearrange("o (i j) -> o i j", j=P), rowparts[0:T, k, :]).then_inc(brow_copied, 16)
                for par in range(2):
                    for a in range(HG):
                        sp.dma_start(q_sb[MAXROWS + k:MAXROWS + k + 1, par, a, :].rearrange("o (i j) -> o i j", j=P),
                                     rowparts[0:T, k, :]).then_inc(brow_copied, 16)
            sp.wait_ge(split_step, 3)
            maxrows(0)

            def group(it, par, more_qk, more_max):
                g = it * 2 + par
                for c in range(NC - 1):
                    store(g, NC * par + c, c, it * (2 * NC) + (NC * par + c + 1))
                if more_max:
                    sp.wait_ge(split_step, it * 6 + (3 * par + 6))
                    maxrows(1 - par)
                if more_qk:
                    sp.wait_ge(st_ready, it * (2 * HG * STEPS) + HG * STEPS * (par + 1))
                    load_qk(g + 2, par)
                store(g, NC * par + 2, 2, it * (2 * NC) + (NC * par + 3))
                if more_qk:
                    sp.wait_ge(pv_done, it * (2 * STEPS) + STEPS * (par + 1))
                    load_v(g + 2, par)

            with sp.Fori(0, NG // 2 - 1) as it:
                group(it, 0, True, True)
                group(it, 1, True, True)
            group(NG // 2 - 1, 0, False, True)
            group(NG // 2 - 1, 1, False, False)
            for i in range(2):
                sp.wait_ge(o_stored[i], 64 * (NG // 2) * NC + 16)
            for i in range(T):
                if i >= 3:
                    sp.wait_ge(ot_ready, 2 * (i - 2))
                sp.dma_start(o_nat[i % 3][0:RP[i], :, :],
                             att[:, P * P * i:P * P * i + P * RP[i]].rearrange("h (r j) -> r h j", j=P)).then_inc(on_loaded[i % 3], 16)
            sp.wait_ge(nat_read, NC * (len(PROPS) + 1))
            full = (KROWS - 1) * T
            sp.dma_start(out[0:full, :].rearrange("(p t) d -> p t d", t=T), nat[0:KROWS - 1, :, :]).then_inc(out_stored, 16)
            sp.dma_start(out[full:N, :], nat[KROWS - 1:KROWS, 0, :]).then_inc(out_stored, 16)
            sp.wait_ge(out_stored, 32)

        @block.gpsimd
        def _(pool):
            nc.gpsimd.memset(ident[:], 0.0).then_inc(s_ident, 1)
            pool.wait_ge(s_ident, 1)
            nc.gpsimd.affine_select(out=ident[:], in_=ident[:], compare_op=ALU.not_equal, fill=1.0, base=0,
                                    pattern=[[-1, P]], channel_multiplier=1).then_inc(s_ident, 1)
            for e in range(2 * T):
                r = RP[e // 2]
                pool.wait_ge(rem1_ready, e + 1)
                nc.gpsimd.tensor_copy(parts[e % 2][0:r, 1, :], rem[e % 2][0:r, :]).then_inc(part2_ready, 1)
            pool.wait_ge(eb_ready, MULS)

            def mults(it, u):
                c, t = divmod(u % STEPS, T)
                pool.wait_ge(exps_done, it * (2 * HG * MULS) + HG * (muls_before(u) + 1))
                w = ring[0:NKEYS[t], u % RING, :, 0:CW[c]]
                e = ebias[0:NKEYS[t], muls_before(u % STEPS), 0:CW[c]].unsqueeze(1).to_broadcast([NKEYS[t], HG, CW[c]])
                nc.gpsimd.tensor_tensor(w, w, e, ALU.mult).then_inc(mults_done, 1)

            with pool.Fori(0, NG // 2) as it:
                for u in range(2 * STEPS):
                    if kind(u) == MUL:
                        mults(it, u)

        @block.scalar
        def _(act):
            for b in range(11):
                act.wait_ge(wt_ready, b + 1)
                if b < 8:
                    dst = wT[:, b // 2, 512 * (b % 2):512 * (b % 2) + 512] if b < 6 else \
                        woT[:, 4 * (b - 6):4 * (b - 6) + 4, :].rearrange("p h d -> p (h d)")
                    nc.scalar.activation(dst, ps[:, b % 8, :], ACT.Copy).then_inc(wt_read, 1)
                else:
                    a = 512 * (b - 8)
                    w = min(512, N - a)
                    nc.scalar.activation(xT[:, a:a + w], ps[:, b % 8, 0:w], ACT.Copy).then_inc(wt_read, 1)
            for i in range(T):
                r = RP[i]
                for w in range(3):
                    s = 3 * i + w
                    src = ps[0:r, 2 * (s % 4):2 * (s % 4) + 2, :].rearrange("p b n -> p (b n)")
                    act.wait_ge(proj_ready, s + 1)
                    if w < 2:
                        e = 2 * i + w
                        sc = SCALE if w == 0 else 1.0
                        if e >= 2:
                            act.wait_ge(part3_ready, e - 1)
                            act.wait_ge(parts_stored[e % 2], 48 * (e // 2))
                        nc.scalar.activation(rem[e % 2][0:r, :], src, ACT.Copy, scale=sc)
                        nc.scalar.activation(parts[e % 2][0:r, 0, :], src, ACT.Copy, scale=sc).then_inc(proj_read, 1)
                    else:
                        if i == 0:
                            act.wait_ge(fill, 1)
                        if i >= 2:
                            act.wait_ge(v_stored[i % 2], 16 * (i // 2))
                        nc.scalar.activation(v_out[i % 2][0:r, :, 0:H].rearrange("p j h -> p h j"),
                                             src.rearrange("p (h j) -> p h j", h=H), ACT.Copy).then_inc(proj_read, 1)
            for i in range(T):
                for b, (t0, nt) in enumerate(TB):
                    n = N_ADJ * i + b
                    act.wait_ge(adjt_ready, n + 1)
                    nc.scalar.activation(adjT[0:KROWS, t0:t0 + nt, P * i:P * i + RP[i]],
                                         ps[0:KROWS, n % 6, :].rearrange("p (t n) -> p t n", n=P)[:, 0:nt, 0:RP[i]],
                                         ACT.Copy).then_inc(adjt_read, 1)
            for m in range(MULS):
                act.wait_ge(eb_sum, m + 1)
                s = [s for s in range(STEPS) if kind(s) == MUL][m]
                e = ebias[0:NKEYS[s % T], m, 0:CW[s // T]]
                nc.scalar.activation(e, e, ACT.Exp).then_inc(eb_ready, 1)

            def exps(it, u):
                c, t = divmod(u % STEPS, T)
                slot = u % RING
                if kind(u) == ADD:
                    return
                if u >= RING or not isinstance(it, int) or it > 0:
                    act.wait_ge(pv_done, it * (2 * STEPS) + (u - RING + 1))
                for a in range(HG):
                    j = HG * u + a
                    act.wait_ge(st_ready, it * (2 * HG * STEPS) + (j + 1))
                    nc.scalar.activation(ring[0:NKEYS[t], slot, a, 0:CW[c]], ps[0:NKEYS[t], ST_BANK + j % 3, 0:CW[c]],
                                         ACT.Exp).then_inc(exps_done, 1)

            def sbexps(it, u):
                if kind(u) != ADD:
                    return
                c, t = divmod(u % STEPS, T)
                act.wait_ge(adds_done, it * (2 * HG * ADDS) + HG * (adds_before(u) + 1))
                w = ring[0:NKEYS[t], u % RING, :, 0:CW[c]]
                nc.scalar.activation(w, w, ACT.Exp).then_inc(sbexp_done, 1)

            def copy_sums(it, q):
                act.wait_ge(pv_done, it * (2 * STEPS) + T * (q + 1))
                act.wait_ge(o_stored[q % 2], it * (64 * NC) + (64 * (q // 2) + 16))
                nc.scalar.activation(o_sb[0:96 + V1, q % 2, 0:CW[q % NC]], ps[0:96 + V1, PV_BANK, 0:CW[q % NC]],
                                     ACT.Copy).then_inc(o_copied, 1)

            for u in range(ACT_LEAD):
                exps(0, u)
                if u:
                    sbexps(0, u - 1)

            def body(it, last):
                for xx in range(2 * STEPS):
                    u = xx + ACT_LEAD
                    if xx % T == T - 1:
                        copy_sums(it, xx // T)
                    if u < 2 * STEPS or not last:
                        exps(it, u)
                    if u - 1 < 2 * STEPS or not last:
                        sbexps(it, u - 1)

            with act.Fori(0, NG // 2 - 1) as it:
                body(it, False)
            body(NG // 2 - 1, True)

            for i in range(T):
                for b in range(2):
                    n = 2 * i + b
                    act.wait_ge(ot_ready, n + 1)
                    nc.scalar.activation(oT[:, 4 * b:4 * b + 4, P * i:P * i + RP[i]],
                                         ps[:, n % 6, :].rearrange("p (h n) -> p h n", n=P)[:, :, 0:RP[i]],
                                         ACT.Copy).then_inc(ot_read, 1)

            def norm(k):
                def std(c):
                    act.wait_ge(var_ready, NC * k + c + 1)
                    nc.scalar.activation(sq[:, C0[c]:C0[c] + CW[c]], ps[:, 7, 0:CW[c]], ACT.Sqrt, bias=epst[:]).then_inc(std_ready, 1)

                for c in range(NC):
                    act.wait_ge(cen_ready, NC * k + c + 1)
                    cs = slice(C0[c], C0[c] + CW[c])
                    nc.scalar.activation(sq[:, cs], cen[:, cs], ACT.Square).then_inc(sq_ready, 1)
                    if c:
                        std(c - 1)
                std(NC - 1)

            def naturals(k, rows):
                for b, (t0, nt) in enumerate(TB):
                    n = NC * k + b
                    act.wait_ge(nat_ready, n + 1)
                    nc.scalar.activation(nat[0:KROWS, t0:t0 + nt, :],
                                         ps[0:KROWS, 5 + b, 0:nt * D].rearrange("p (t d) -> p t d", d=D),
                                         ACT.Copy).then_inc(nat_read, 1)

            norm(0)
            dense = 0
            for k, (src, layers, fn) in enumerate(PROPS):
                naturals(k, None)
                for st, c in wave(len(layers)):
                    cs = slice(C0[c], C0[c] + CW[c])
                    if st == 0:
                        act.wait_ge(agg_ready, NC * k + c + 1)
                        nc.scalar.activation(z_sb[:, cs], ps[:, c, 0:CW[c]], ACT.Copy).then_inc(agg_read, 1)
                        continue
                    act.wait_ge(dense_ready, dense + 1)
                    src_ps = ps[:, 3 + dense % 2, 0:CW[c]]
                    b = bia[:, layers[st - 1]:layers[st - 1] + 1]
                    if fn == "leaky":
                        nc.scalar.activation(leak[:, cs], src_ps, ACT.Identity, bias=b).then_inc(act_done, 1)
                    else:
                        nc.scalar.activation(out_sb[:, cs], src_ps, ACT.Silu if fn == "silu" else ACT.Relu, bias=b).then_inc(act_done, 1)
                    dense += 1
                if k in NORM_AFTER:
                    norm(NORM_AFTER[k])
            naturals(len(PROPS), None)

        @block.vector
        def _(dve):
            def third(e):
                r = RP[e // 2]
                dve.wait_ge(part2_ready, e + 1)
                nc.vector.tensor_tensor(parts[e % 2][0:r, 2, :], rem[e % 2][0:r, :], parts[e % 2][0:r, 1, :],
                                        ALU.subtract).then_inc(part3_ready, 1)

            nc.vector.memset(v_out[0][:, :, H:V1], 1.0)
            nc.vector.memset(v_out[1][:, :, H:V1], 1.0)
            nc.vector.memset(avg[:], 1.0 / D)
            nc.vector.memset(epst[:], EPS)
            nc.vector.memset(ones3[:], 1.0)
            nc.vector.memset(xT[:, N:NPAD], 0.0).then_inc(fill, 1)
            nc.vector.memset(q_sb[0:64, :, :, N:NPAD], 0.0)
            nc.vector.memset(q_sb[64:96, :, :, :], 0.0).then_inc(fill, 1)
            nc.vector.memset(k_sb[64:96, :, :, :], 0.0)
            nc.vector.memset(k_sb[96:128, :, :, :], 1.0).then_inc(fill, 1)
            nc.vector.memset(v_sb[:], 0.0).then_inc(fill, 1)
            for i in range(2):
                nc.vector.memset(o_sb[:, i, :], 0.0).then_inc(o_stored[i], 16)
            dve.wait_ge(wt_ready, 11)
            for i in range(2):
                nc.vector.memset(adj_nat[i][:, N:NPAD], 0.0).then_inc(fill, 1)
            for e in range(2 * T):
                i, w = divmod(e, 2)
                r = RP[i]
                dve.wait_ge(proj_read, 3 * i + w + 1)
                nc.vector.tensor_tensor(rem[e % 2][0:r, :], rem[e % 2][0:r, :], parts[e % 2][0:r, 0, :],
                                        ALU.subtract).then_inc(rem1_ready, 1)
                if e:
                    third(e - 1)
            third(2 * T - 1)
            nc.vector.memset(negmax[:], 0.0).then_inc(pv_clear, 1)
            dve.wait_ge(pv_clear, 1)
            for i in range(T):
                dve.wait_ge(adj_loaded[i % 2], 16 * (i // 2 + 1))
                nc.vector.tensor_reduce(negmax[0:RP[i], i:i + 1], adj_nat[i % 2][0:RP[i], 0:N], op=ALU.max,
                                        axis=AX.X, negate=True).then_inc(bmax_ready, 1)
            dve.wait_ge(brow_ready, 1)
            nc.vector.tensor_scalar(rowparts[0:T, 0, :], ps[0:T, 6, 0:P], 2.0, None, ALU.mult).then_inc(brow_step, 1)
            dve.wait_ge(brow_step, 1)
            nc.vector.scalar_tensor_tensor(out=rowrem[0:T, :], in0=ps[0:T, 6, 0:P], scalar=2.0, in1=rowparts[0:T, 0, :],
                                           op0=ALU.mult, op1=ALU.subtract).then_inc(brow_step, 1)
            dve.wait_ge(brow_step, 2)
            nc.vector.tensor_copy(rowparts[0:T, 1, :], rowrem[0:T, :]).then_inc(brow_step, 1)
            dve.wait_ge(brow_step, 3)
            nc.vector.tensor_tensor(rowparts[0:T, 2, :], rowrem[0:T, :], rowparts[0:T, 1, :], ALU.subtract).then_inc(brow_step, 1)
            dve.wait_ge(v_stored[1], 16 * len(range(1, T, 2)))
            dve.wait_ge(adjt_read, N_ADJ * T)
            for m, s in enumerate(s for s in range(STEPS) if kind(s) == MUL):
                c, t = divmod(s, T)
                dve.wait_ge(bb_ready, c + 1)
                nc.vector.scalar_tensor_tensor(out=ebias[0:NKEYS[t], m, 0:CW[c]], in0=adjT[0:NKEYS[t], t, C0[c]:C0[c] + CW[c]],
                                               scalar=2.0, in1=ps[0:NKEYS[t], c, 0:CW[c]], op0=ALU.mult,
                                               op1=ALU.add).then_inc(eb_sum, 1)
            nc.vector.memset(ps[:, PV_BANK, :], 0.0).then_inc(o_copied, 1)

            def max_pair(it, gbase, p):
                sl = SLOTS * gbase + p
                b = 2 * (sl % 2)
                dve.wait_ge(s_ready, it * (2 * SLOTS) + (sl + 1))
                nc.vector.tensor_reduce(maxes[:, 2 * p:2 * p + 2], ps[:, b:b + 2, 0:MW], op=ALU.max,
                                        axis=AX.X).then_inc(s_read, 1)

            def group_max(it, gbase):
                dve.wait_ge(s_read, it * (2 * SLOTS) + (SLOTS * gbase + PAIRS))
                nc.vector.tensor_reduce(negmax[:, 0:HG * T], maxes[:].rearrange("p (x c) -> p x c", c=NC), op=ALU.max, axis=AX.X,
                                        negate=True).then_inc(negmax_ready, 1)

            def split_max(it, gbase, first=False):
                sl = SLOTS * gbase + PAIRS
                src = ps[0:HG * T, 2 * (sl % 2), 0:P]
                dve.wait_ge(s_ready, it * (2 * SLOTS) + (sl + 1))
                if first:
                    dve.wait_ge(brow_copied, 16 * PARTS * (1 + 2 * HG))
                else:
                    dve.wait_ge(maxrow_loaded[(gbase - 1) % 2], it * 48 + 48 * ((gbase - 1) // 2 + 1))
                nc.vector.tensor_copy(rowparts[:, 0, :], src).then_inc(split_step, 1)
                dve.wait_ge(split_step, it * 6 + (3 * gbase + 1))
                nc.vector.tensor_tensor(rowrem[:], src, rowparts[:, 0, :], ALU.subtract).then_inc(s_read, 1)
                dve.wait_ge(s_read, it * (2 * SLOTS) + (sl + 1))
                nc.vector.tensor_copy(rowparts[:, 1, :], rowrem[:]).then_inc(split_step, 1)
                dve.wait_ge(split_step, it * 6 + (3 * gbase + 2))
                nc.vector.tensor_tensor(rowparts[:, 2, :], rowrem[:], rowparts[:, 1, :], ALU.subtract).then_inc(split_step, 1)

            for p in range(PAIRS):
                max_pair(0, 0, p)
            group_max(0, 0)
            split_max(0, 0, True)

            def add_bias(it, u, a):
                c, t = divmod(u % STEPS, T)
                if a == 0 and (u >= RING or not isinstance(it, int) or it > 0):
                    dve.wait_ge(pv_done, it * (2 * STEPS) + (u - RING + 1))
                j = HG * u + a
                dve.wait_ge(st_ready, it * (2 * HG * STEPS) + (j + 1))
                nc.vector.scalar_tensor_tensor(
                    out=ring[0:NKEYS[t], u % RING, a, 0:CW[c]], in0=adjT[0:NKEYS[t], t, C0[c]:C0[c] + CW[c]],
                    scalar=2.0, in1=ps[0:NKEYS[t], ST_BANK + j % 3, 0:CW[c]], op0=ALU.mult,
                    op1=ALU.add).then_inc(adds_done, 1)

            def step(it, u, maxing):
                s = u % STEPS
                nxt = u // STEPS + 1
                pairs = list(range(PAIR_FROM[s], PAIR_FROM[s] + PAIRS_AT[s])) if maxing else []
                for a in range(HG):
                    if a % 2 == 0 and pairs:
                        max_pair(it, nxt, pairs.pop(0))
                    if kind(u) == ADD:
                        add_bias(it, u, a)
                for p in pairs:
                    max_pair(it, nxt, p)
                if maxing and s == S_LAST:
                    group_max(it, nxt)
                if maxing and s == S_LAST + 1:
                    split_max(it, nxt)

            for u in range(DVE_LEAD):
                step(0, u, True)
            with dve.Fori(0, NG // 2 - 1) as it:
                for xx in range(2 * STEPS):
                    step(it, xx + DVE_LEAD, True)
            for u in range(DVE_LEAD, 2 * STEPS):
                step(NG // 2 - 1, u, u < STEPS)

            for i in range(T):
                r = RP[i]
                dve.wait_ge(on_loaded[i % 3], 16 * (i // 3 + 1))
                o = o_nat[i % 3]
                if i >= 2:
                    dve.wait_ge(on_ready, i - 1)
                nc.vector.reciprocal(rsum[i % 2][0:r, :], o[0:r, H, :]).then_inc(rsum_ready, 1)
                dve.wait_ge(rsum_ready, i + 1)
                nc.vector.tensor_tensor(o[0:r, 0:H, :], o[0:r, 0:H, :], rsum[i % 2][0:r, :].unsqueeze(1).to_broadcast([r, H, P]),
                                        ALU.mult).then_inc(on_ready, 1)

            def norm(k, layer_chunk):
                def close(c):
                    cs = slice(C0[c], C0[c] + CW[c])
                    dve.wait_ge(std_ready, NC * k + c + 1)
                    nc.vector.reciprocal(sq[:, cs], sq[:, cs]).then_inc(inv_ready, 1)
                    dve.wait_ge(inv_ready, NC * k + c + 1)
                    nc.vector.tensor_tensor(xT[:, cs], cen[:, cs], sq[:, cs], ALU.mult).then_inc(x_ready, 1)

                for c in range(NC):
                    cs = slice(C0[c], C0[c] + CW[c])
                    y = layer_chunk(c)
                    nc.vector.tensor_tensor(z_sb[:, cs], y, xT[:, cs], ALU.add).then_inc(z_ready, 1)
                for c in range(NC):
                    cs = slice(C0[c], C0[c] + CW[c])
                    dve.wait_ge(mean_ready, NC * k + c + 1)
                    nc.vector.tensor_tensor(cen[:, cs], z_sb[:, cs], ps[:, 5 + c % 2, 0:CW[c]], ALU.subtract).then_inc(cen_ready, 1)
                for c in range(NC):
                    close(c)

            def projected(c):
                dve.wait_ge(y_ready, c + 1)
                return ps[:, 6 + c % 2, 0:CW[c]] if c < 2 else ps[:, 0, 0:CW[c]]

            dve.wait_ge(y_ready, 1)
            nc.vector.memset(out_sb[:, N:NPAD], 0.0)
            norm(0, projected)
            dense = 0
            lk = 0
            for k, (src, layers, fn) in enumerate(PROPS):
                for st, c in wave(len(layers)):
                    if st == 0:
                        continue
                    dense += 1
                    if fn == "leaky":
                        cs = slice(C0[c], C0[c] + CW[c])
                        dst = out_sb if st == len(layers) else mid[st - 1]
                        dve.wait_ge(act_done, dense)
                        nc.vector.scalar_tensor_tensor(out=dst[:, cs], in0=leak[:, cs], scalar=0.01, in1=leak[:, cs],
                                                       op0=ALU.mult, op1=ALU.max).then_inc(leaky_done, 1)
                        lk += 1
                if k in NORM_AFTER:
                    if fn == "leaky":
                        dve.wait_ge(leaky_done, lk)
                    dve.wait_ge(act_done, dense)
                    norm(NORM_AFTER[k], lambda c: out_sb[:, C0[c]:C0[c] + CW[c]])

        @block.tensor
        def _(pe):
            pe.wait_ge(s_ident, 2)
            pe.wait_ge(w_loaded, 64)
            pe.wait_ge(x_loaded, 32)
            for b in range(11):
                if b >= 8:
                    pe.wait_ge(wt_read, b - 7)
                for q in range(4):
                    if b < 6:
                        src = w_nat[:, b // 2, 4 * (b % 2) + q, :]
                    elif b < 8:
                        src = w_nat[:, 3, :, :].rearrange("p h d -> p (h d)").rearrange("p (j h) -> p h j", h=H)[:, 4 * (b - 6) + q, :]
                    elif 4 * (b - 8) + q < T:
                        src = x_nat[0:RP[4 * (b - 8) + q], 4 * (b - 8) + q, :]
                    else:
                        continue
                    r = src.shape[0]
                    last = nc.tensor.transpose(ps[:, b % 8, P * q:P * q + r], src, ident[0:r, 0:r])
                last.then_inc(wt_ready, 1)
            pe.wait_ge(wt_read, 11)
            for i in range(T):
                for w in range(3):
                    s = 3 * i + w
                    if s >= 4:
                        pe.wait_ge(proj_read, s - 3)
                    for h in range(2):
                        last = nc.tensor.matmul(ps[0:RP[i], 2 * (s % 4) + h, :], xT[:, P * i:P * i + RP[i]],
                                                wT[:, w, 512 * h:512 * h + 512], start=True, stop=True)
                    last.then_inc(proj_ready, 1)
            pe.wait_ge(proj_read, 3 * T)
            for i in range(T):
                pe.wait_ge(adj_loaded[i % 2], 16 * (i // 2 + 1))
                if i == 0:
                    pe.wait_ge(fill, 6)
                cols = adj_nat[i % 2][0:RP[i], 0:T * KROWS].rearrange("p (m t) -> p t m", t=T)
                for b, (t0, nt) in enumerate(TB):
                    n = N_ADJ * i + b
                    if n >= 6:
                        pe.wait_ge(adjt_read, n - 5)
                    for t in range(t0, t0 + nt):
                        last = nc.tensor.transpose(ps[0:KROWS, n % 6, P * (t - t0):P * (t - t0) + RP[i]], cols[:, t, :],
                                                   ident[0:RP[i], 0:RP[i]])
                    last.then_inc(adjt_ready, 1)
            pe.wait_ge(bmax_ready, T)
            nc.tensor.transpose(ps[:, 6, 0:P], negmax[:], ident[:]).then_inc(brow_ready, 1)
            pe.wait_ge(brow_copied, 16 * PARTS * (1 + 2 * HG))
            pe.wait_ge(adjt_read, N_ADJ * T)
            for c in range(NC):
                nc.tensor.matmul(ps[0:KROWS, c, 0:CW[c]], ones3[:], biasrow[:, C0[c]:C0[c] + CW[c]], start=True,
                                 stop=True).then_inc(bb_ready, 1)

            def score_pair(it, gbase, p):
                par = gbase % 2
                sl = SLOTS * gbase + p
                if not (isinstance(it, int) and it == 0 and sl < 2):
                    pe.wait_ge(s_read, it * (2 * SLOTS) + (sl - 1))
                if p == 0:
                    pe.wait_ge(qk_loaded[par], it * 192 + 192 * (gbase // 2 + 1))
                for e in range(2):
                    a, rest = divmod(2 * p + e, T * NC)
                    i, c = divmod(rest, NC)
                    last = nc.tensor.matmul(ps[:, 2 * (sl % 2) + e, 0:MW], q_sb[0:ZROWS, par, a, P * i:P * i + P],
                                            k_sb[0:ZROWS, par, a, M0[c]:M0[c] + MW], start=True, stop=True)
                last.then_inc(s_ready, 1)

            def turn_max(it, gbase):
                sl = SLOTS * gbase + PAIRS
                pe.wait_ge(s_read, it * (2 * SLOTS) + (sl - 1))
                pe.wait_ge(negmax_ready, it * 2 + (gbase + 1))
                nc.tensor.transpose(ps[:, 2 * (sl % 2), 0:P], negmax[:], ident[:]).then_inc(s_ready, 1)

            def scores(it, u, a):
                s = u % STEPS
                par = u // STEPS % 2
                c, t = divmod(s, T)
                rows = MAXROWS if kind(u) == MUL else ALLROWS
                if s == 0 and a == 0:
                    pe.wait_ge(maxrow_loaded[par], it * 48 + 48 * (u // (2 * STEPS) + 1))
                j = HG * u + a
                jb = j - 3
                if jb >= 0 or not isinstance(it, int) or it > 0:
                    ub = jb // HG
                    if kind(ub) == MUL:
                        pe.wait_ge(exps_done, it * (2 * HG * MULS) + (HG * muls_before(ub) + jb % HG + 1))
                    else:
                        pe.wait_ge(adds_done, it * (2 * HG * ADDS) + (HG * adds_before(ub) + jb % HG + 1))
                nc.tensor.matmul(ps[0:NKEYS[t], ST_BANK + j % 3, 0:CW[c]],
                                 k_sb[0:rows, par, a, t:t + T * (NKEYS[t] - 1) + 1:T],
                                 q_sb[0:rows, par, a, C0[c]:C0[c] + CW[c]], start=True, stop=True).then_inc(st_ready, 1)

            def values(it, u):
                s = u % STEPS
                par = u // STEPS % 2
                c, t = divmod(s, T)
                if kind(u) == MUL:
                    pe.wait_ge(mults_done, it * (2 * MULS) + (muls_before(u) + 1))
                else:
                    pe.wait_ge(sbexp_done, it * (2 * ADDS) + (adds_before(u) + 1))
                if s == 0:
                    pe.wait_ge(v_loaded[par], it * 32 + 32)
                if t == 0:
                    pe.wait_ge(o_copied, it * (2 * NC) + (u // T + 1))
                r = NKEYS[t]
                for a in range(HG):
                    last = nc.tensor.matmul(ps[32 * a:32 * a + V1, PV_BANK, 0:CW[c]], v_sb[0:r, par, a, V1 * t:V1 * t + V1],
                                            ring[0:r, u % RING, a, 0:CW[c]], start=(t == 0), stop=(t == T - 1))
                last.then_inc(pv_done, 1)

            def step(it, u, maxing, scoring, with_values):
                s = u % STEPS
                nxt = u // STEPS + 1
                pairs = list(range(PAIR_FROM[s], PAIR_FROM[s] + PAIRS_AT[s])) if maxing else []
                for a in range(HG):
                    if a % 2 == 0 and pairs:
                        score_pair(it, nxt, pairs.pop(0))
                    if scoring:
                        scores(it, u, a)
                if with_values:
                    values(it, u - LAG)
                for p in pairs:
                    score_pair(it, nxt, p)
                if maxing and s == S_LAST + 1:
                    turn_max(it, nxt)

            pe.wait_ge(eb_sum, MULS)
            pe.wait_ge(brow_step, 2)
            for p in range(PAIRS):
                score_pair(0, 0, p)
            turn_max(0, 0)
            for u in range(LAG):
                step(0, u, True, True, False)
            with pe.Fori(0, NG // 2 - 1) as it:
                for xx in range(2 * STEPS):
                    step(it, xx + LAG, True, True, True)
            for u in range(LAG, 2 * STEPS + LAG):
                step(NG // 2 - 1, u, u < STEPS, u < 2 * STEPS, True)

            for i in range(T):
                pe.wait_ge(on_ready, i + 1)
                if i == 0:
                    pe.wait_ge(o_copied, NC * NG + 1)
                for b in range(2):
                    n = 2 * i + b
                    if n >= 6:
                        pe.wait_ge(ot_read, n - 5)
                    for h in range(4):
                        last = nc.tensor.transpose(ps[:, n % 6, P * h:P * h + RP[i]], o_nat[i % 3][0:RP[i], 4 * b + h, :],
                                                   ident[0:RP[i], 0:RP[i]])
                    last.then_inc(ot_ready, 1)
            pe.wait_ge(ot_read, 2 * T)
            for c in range(NC):
                dst = ps[:, 6 + c % 2, 0:CW[c]] if c < 2 else ps[:, 0, 0:CW[c]]
                for h in range(H):
                    last = nc.tensor.matmul(dst, woT[:, h, :], oT[:, h, C0[c]:C0[c] + CW[c]], start=(h == 0), stop=(h == H - 1))
                last.then_inc(y_ready, 1)

            def norm(k):
                def var(c):
                    pe.wait_ge(sq_ready, NC * k + c + 1)
                    if c:
                        pe.wait_ge(std_ready, NC * k + c)
                    nc.tensor.matmul(ps[:, 7, 0:CW[c]], avg[:], sq[:, C0[c]:C0[c] + CW[c]], start=True, stop=True).then_inc(var_ready, 1)

                pe.wait_ge(z_ready, NC * k + NC)
                for c in range(NC):
                    if c == 2:
                        pe.wait_ge(cen_ready, NC * k + 1)
                    nc.tensor.matmul(ps[:, 5 + c % 2, 0:CW[c]], avg[:], z_sb[:, C0[c]:C0[c] + CW[c]], start=True, stop=True).then_inc(mean_ready, 1)
                    if c:
                        var(c - 1)
                var(NC - 1)

            def naturals(k, src):
                cols = src[:, 0:T * KROWS].rearrange("p (m t) -> p t m", t=T)
                for b, (t0, nt) in enumerate(TB):
                    for t in range(t0, t0 + nt):
                        last = nc.tensor.transpose(ps[0:KROWS, 5 + b, P * (t - t0):P * (t - t0) + D], cols[:, t, :], ident[:])
                    last.then_inc(nat_ready, 1)

            pe.wait_ge(small_loaded, 256)
            norm(0)
            dense = 0
            norms = 1
            for k, (src, layers, fn) in enumerate(PROPS):
                if src == "x":
                    pe.wait_ge(x_ready, NC * norms)
                elif fn == "leaky":
                    pe.wait_ge(leaky_done, lk_before(dense))
                else:
                    pe.wait_ge(act_done, dense)
                naturals(k, xT if src == "x" else out_sb)
                for st, c in wave(len(layers)):
                    cs = slice(C0[c], C0[c] + CW[c])
                    if st == 0:
                        if k and c == 0:
                            pe.wait_ge(agg_read, NC * k)
                        for t in range(T):
                            if c == 0 and t in (0, 4, 8):
                                pe.wait_ge(nat_read, NC * k + t // 4 + 1)
                            last = nc.tensor.matmul(ps[:, c, 0:CW[c]], nat[0:KROWS, t, :], adjT[0:KROWS, t, cs],
                                                    start=(t == 0), stop=(t == T - 1))
                        last.then_inc(agg_ready, 1)
                        continue
                    if st == 1:
                        pe.wait_ge(agg_read, NC * k + c + 1)
                        rhs = z_sb
                    else:
                        pe.wait_ge(leaky_done, lk_before(dense_index(k, st - 1, c)) + 1)
                        rhs = mid[st - 2]
                    if dense >= 2:
                        pe.wait_ge(act_done, dense - 1)
                    nc.tensor.matmul(ps[:, 3 + dense % 2, 0:CW[c]], wts[:, layers[st - 1], :], rhs[:, cs], start=True,
                                     stop=True).then_inc(dense_ready, 1)
                    dense += 1
                if k in NORM_AFTER:
                    norm(NORM_AFTER[k])
                    norms += 1
            pe.wait_ge(x_ready, NC * norms)
            naturals(len(PROPS), xT)


def dense_index(k, st, c):
    before = sum(NC * len(layers) for _, layers, _ in PROPS[:k])
    order = [x for x in wave(len(PROPS[k][1])) if x[0]]
    return before + order.index((st, c))


def lk_before(dense):
    n = 0
    total = 0
    for _, layers, fn in PROPS:
        size = NC * len(layers)
        take = min(size, max(0, dense - total))
        if fn == "leaky":
            n += take
        total += size
    return n


_WEIGHTS = ["L1_gnn_W", "L2_gnn_kernel"] + [f"L3_gnn_{d}_W{i}" for d in ("uv", "vu") for i in (1, 2, 3)]
_BIASES = ["L1_gnn_b", "L2_gnn_bias"] + [f"L3_gnn_{d}_b{i}" for d in ("uv", "vu") for i in (1, 2, 3)]


def kernel(**inputs):
    import numpy as np
    import concourse.bacc as bacc
    from concourse.bass_utils import run_bass_kernel_spmd

    nc = bacc.Bacc("TRN2", target_bir_lowering=False, num_devices=1)
    arrays = {}

    def arg(name):
        a = np.ascontiguousarray(inputs[name])
        arrays["in_" + name] = a
        return nc.dram_tensor("in_" + name, a.shape, mybir.dt.from_np(a.dtype), kind="ExternalInput").ap()

    x, adj = arg("x"), arg("adj")
    wqkv = [arg("L0_gnn_W" + n) for n in "qkv"]
    wo = arg("L0_gnn_Wo")
    weights = [arg(n) for n in _WEIGHTS]
    biases = [arg(n) for n in _BIASES]
    out = nc.dram_tensor("out", (N, D), F32, kind="ExternalOutput").ap()
    build(nc, x, adj, wqkv, wo, weights, biases, out)
    r = run_bass_kernel_spmd(nc, [arrays], core_ids=[0])
    return r.results[0]["out"]
```

```python
from contextlib import ExitStack

import concourse.bass as bass
from concourse import mybir

F32 = mybir.dt.float32
BF16 = mybir.dt.bfloat16
ALU = mybir.AluOpType
ACT = mybir.ActivationFunctionType
AX = mybir.AxisListType

N = 1354
D = 128
H = 8
P = 128
T = -(-N // P)
NPAD = T * P
KROWS = -(-N // T)
NKEYS = [KROWS if t < N - T * (KROWS - 1) else KROWS - 1 for t in range(T)]
RP = [min(P, N - P * i) for i in range(T)]
G = N * D
SCALE = float(D) ** -0.5
EPS = 1e-5

HG = 4
NG = D // HG
CW = [452, 452, 450]
C0 = [0, 452, 904]
MW = 452
M0 = [0, 451, 902]
NC = len(CW)
STEPS = NC * T
PAIRS = HG * T * NC // 2
BATCHES = [(0, 4), (4, 4), (8, T - 8)]
SLOTS = PAIRS + len(BATCHES)
PARTS = 3
SPLITS = 3
SROWS = PARTS * PARTS * H
ZROWS = 96
MAXROWS = ZROWS + PARTS
ALLROWS = MAXROWS + PARTS
V1 = H + 1

RING = 6
LAG = 4
ACT_LEAD = RING
DVE_LEAD = RING
AHEAD = 17
ADD, MUL, PE = "a", "m", "p"
KIND = "mammammammamammammammamammammamma"
assert len(KIND) == STEPS
A_PAIRS, P_PAIRS = 0, 4
STEP_PAIRS = {ADD: A_PAIRS, PE: P_PAIRS}
_fixed = sum(STEP_PAIRS.get(x, 0) for x in KIND)
_rest = PAIRS - _fixed
_muls = KIND.count(MUL)
PAIRS_IN = []
for _s, _k in enumerate(KIND):
    _m = KIND[:_s].count(MUL)
    PAIRS_IN.append(STEP_PAIRS[_k] if _k != MUL else (_m + 1) * _rest // _muls - _m * _rest // _muls)
PASS_PAIRS = [PAIRS_IN[(w - AHEAD) % STEPS] for w in range(STEPS)]
PAIR_FROM = [sum(PASS_PAIRS[:w]) for w in range(STEPS + 1)]
BATCH_END = [next(w for w in range(STEPS) if 2 * PAIR_FROM[w] >= (i + n) * HG * NC) for i, n in BATCHES[:-1]] + [STEPS]
ADDS = KIND.count(ADD)
EXPS = STEPS - ADDS
MULS = KIND.count(MUL)


A_PLANS = ["0123V", "01P23V", "0P12P3V"]
M_PLANS = ["0123V", "0P123V", "P01P23V", "P01P2P3V", "P0P1P2P3V"]
P_PLANS = ["0123V", "01P23V", "0P12P3V", "0P1P2P3V", "0P1P2P3PV"]
PLANS = {ADD: A_PLANS, MUL: M_PLANS, PE: P_PLANS}


def slot_of(z):
    g, w = divmod(z, STEPS)
    return 0 if z == 0 else SLOTS * g + PAIR_FROM[w] + sum(w > e for e in [0] + BATCH_END[:-1]) - 1


def batch_before(z):
    g, w = divmod(z, STEPS)
    if z and w == 0:
        return len(BATCHES) * g - 1
    return len(BATCHES) * g + BATCH_END.index(w) if w in BATCH_END else None


def plan(u, maxing):
    p = 9
    items = []
    for x in PLANS[kind(u)][PAIRS_IN[u % STEPS]]:
        if x != "P":
            items.append(x)
        elif maxing:
            p += 1
            items.append(p)
    return items


def adds_before(u):
    return u // STEPS * ADDS + KIND[: u % STEPS].count(ADD)


def muls_before(u):
    return u // STEPS * MULS + KIND[: u % STEPS].count(MUL)


def exps_before(u):
    return u // STEPS * (STEPS - ADDS) + (u % STEPS - KIND[: u % STEPS].count(ADD))


def slot(u):
    return u % (2 * STEPS) % RING


def last_user(u):
    return next(v for v in range(u - 1, u - 2 * RING - 1, -1) if slot(v) == slot(u))


def kind(u):
    return KIND[u % STEPS]


UV, VU = (2, 3, 4), (5, 6, 7)
PROPS = [("x", (0,), "silu"), ("out", (0,), "silu"), ("x", (1,), "relu"),
         ("x", UV, "leaky"), ("out", VU, "leaky"), ("out", UV, "leaky"), ("out", VU, "leaky"), ("out", UV, "leaky")]
NORM_AFTER = {1: 1, 2: 2, 7: 3}


def wave(layers):
    return [(st, c - st) for c in range(NC + layers) for st in range(layers + 1) if 0 <= c - st < NC]


def build(nc, x, adj, wqkv, wo, weights, biases, out):
    ctx = ExitStack()
    with ctx:
        def sem(name):
            return ctx.enter_context(nc.semaphore(name))

        def sb(name, shape, dt):
            return ctx.enter_context(nc.sbuf_tensor(name, shape, dt))

        qk_parts = nc.dram_tensor("qk_parts", [2, PARTS, H, G], BF16, kind="Internal").ap()
        v_rows = nc.dram_tensor("v_rows", [G * V1], F32, kind="Internal").ap()
        x_cols = nc.dram_tensor("x_cols", [D, N], F32, kind="Internal").ap()
        max_rows = [nc.dram_tensor(f"max_rows{b}", [PARTS, HG * n, P], BF16, kind="Internal").ap()
                    for b, (_, n) in enumerate(BATCHES)]
        att = nc.dram_tensor("att", [V1, G], F32, kind="Internal").ap()

        adjT = sb("adjT", [P, T, N], F32)
        ident = sb("ident", [P, P], F32)
        ident2 = sb("ident2", [P, P], F32)
        v_sb = sb("v_sb", [P, 2, HG, T * V1], F32)
        o_sb = sb("o_sb", [P, 2, 452], F32)
        maxes = sb("maxes", [P, 2 * PAIRS], F32)
        negmax = sb("negmax", [P, P], F32)
        rowrem = sb("rowrem", [16, P], F32)
        rowparts = sb("rowparts", [16, len(BATCHES), PARTS, P], BF16)
        biasrow = sb("biasrow", [PARTS, NPAD], BF16)
        ones3 = sb("ones3", [PARTS, KROWS], BF16)
        epst = sb("epst", [P, 1], F32)
        avg = sb("avg", [P, P], F32)

        EBSZ = MULS * 452
        QSZ, KSZ = 2 * HG * NPAD // 2, 2 * HG * N // 2
        RSZ = RING * HG * 452
        arena = sb("arena", [P, EBSZ + QSZ + KSZ + RSZ], F32)
        EB0, Q0, K0, R0 = 0, EBSZ, EBSZ + QSZ, EBSZ + QSZ + KSZ

        def carve(at, shape, rows=P, dt=F32):
            size = 1
            for n in shape:
                size *= n
            words = size if dt == F32 else size // 2
            v = arena[0:rows, at:at + words]
            if dt != F32:
                v = v.bitcast(dt)
            if len(shape) == 1:
                return v
            names = "abcd"[: len(shape)]
            return v.rearrange(f"p ({' '.join(names)}) -> p {' '.join(names)}",
                               **{k: n for k, n in zip(names, shape)})

        ebias = carve(EB0, [MULS, 452])
        q_sb = carve(Q0, [2, HG, NPAD], P, BF16)
        k_sb = carve(K0, [2, HG, N], P, BF16)
        ring = carve(R0, [RING, HG, 452])

        x_nat = carve(EB0, [T, D])
        wT = carve(EB0 + T * D, [3, 1024])
        rem = [carve(EB0 + T * D + 3072 + 1024 * i, [1024]) for i in range(SPLITS)]
        w_nat = carve(R0, [3, H, D])
        parts = [carve(R0 + 3072 + 1536 * i, [PARTS, 1024], P, BF16) for i in range(SPLITS)]
        VO0, VO1 = 3072 + 1536 * SPLITS, T * D + 3072 + 1024 * SPLITS
        v_out = [carve(R0 + VO0, [P, V1]), carve(EB0 + VO1, [P, V1])]
        xT0 = carve(R0 + VO0 + P * V1, [NPAD])
        adj_nat = [carve(R0 + NPAD * i, [NPAD]) for i in range(2)]
        assert VO0 + P * V1 + NPAD <= RSZ and VO1 + P * V1 <= EBSZ and 2 * NPAD <= 3072

        at = 0
        oT = carve(0, [H, N]); at += H * N
        o_nat = [carve(at + V1 * P * i, [V1, P]) for i in range(3)]; at += 3 * V1 * P
        rsum = [carve(at + P * i, [P]) for i in range(2)]; at += 2 * P
        z_sb = carve(at, [N]); at += N
        mid = [carve(at + N * i, [N]) for i in range(2)]; at += 2 * N
        leak = carve(at, [N]); at += N
        out_sb = carve(at, [NPAD]); at += NPAD
        cen = carve(at, [N]); at += N
        sq = carve(at, [N]); at += N
        nat = carve(at, [T, D]); at += T * D
        xT = carve(at, [NPAD]); at += NPAD
        wo_nat = carve(at, [D * H]); at += D * H
        woT = carve(at, [H, D]); at += H * D
        wts = carve(at, [8, D]); at += 8 * D
        bia = carve(at, [8]); at += 8
        assert at <= EBSZ + QSZ + KSZ + RSZ

        ps = ctx.enter_context(nc.psum_tensor("ps", [P, 8, 512], F32))
        ST_BANK, PV_BANK = 4, 7

        s_ident = sem("s_ident")
        w_loaded = [sem(f"w_loaded{i}") for i in range(3)]
        x_loaded = sem("x_loaded")
        small_loaded = sem("small_loaded")
        fill = sem("fill")
        spare_rows = sem("spare_rows")
        wt_ready = sem("wt_ready")
        wt_read = sem("wt_read")
        proj_ready = sem("proj_ready")
        proj_read = sem("proj_read")
        rem1_ready = sem("rem1_ready")
        part2_ready = sem("part2_ready")
        part3_ready = sem("part3_ready")
        parts_stored = [sem(f"parts_stored{i}") for i in range(SPLITS)]
        v_stored = [sem(f"v_stored{i}") for i in range(2)]
        adj_loaded = [sem(f"adj_loaded{i}") for i in range(2)]
        adjt_ready = sem("adjt_ready")
        adjt_read = sem("adjt_read")
        bmax_ready = sem("bmax_ready")
        brow_ready = sem("brow_ready")
        brow_step = sem("brow_step")
        brow_copied = sem("brow_copied")
        brow_spread = sem("brow_spread")
        bb_ready = sem("bb_ready")
        eb_sum = sem("eb_sum")
        eb_ready = sem("eb_ready")
        pv_clear = sem("pv_clear")
        qk_loaded = [sem(f"qk_loaded{i}") for i in range(2)]
        v_loaded = [sem(f"v_loaded{i}") for i in range(2)]
        maxrow_loaded = [sem(f"maxrow_loaded{i}") for i in range(len(BATCHES))]
        maxrow_stored = sem("maxrow_stored")
        s_ready = sem("s_ready")
        s_read = sem("s_read")
        negmax_ready = sem("negmax_ready")
        split_step = sem("split_step")
        st_ready = sem("st_ready")
        exps_done = sem("exps_done")
        adds_done = sem("adds_done")
        sbexp_done = sem("sbexp_done")
        mults_done = sem("mults_done")
        pv_done = sem("pv_done")
        o_copied = sem("o_copied")
        o_stored = [sem(f"o_stored{i}") for i in range(2)]
        xt_stored = sem("xt_stored")
        xt_loaded = sem("xt_loaded")
        wo_loaded = sem("wo_loaded")
        wot_ready = sem("wot_ready")
        wot_read = sem("wot_read")
        on_loaded = [sem(f"on_loaded{i}") for i in range(3)]
        rsum_ready = sem("rsum_ready")
        on_ready = sem("on_ready")
        ot_ready = sem("ot_ready")
        ot_read = sem("ot_read")
        y_ready = sem("y_ready")
        z_ready = sem("z_ready")
        mean_ready = sem("mean_ready")
        cen_ready = sem("cen_ready")
        sq_ready = sem("sq_ready")
        var_ready = sem("var_ready")
        std_ready = sem("std_ready")
        inv_ready = sem("inv_ready")
        x_ready = sem("x_ready")
        nat_ready = sem("nat_ready")
        nat_read = sem("nat_read")
        agg_ready = sem("agg_ready")
        agg_read = sem("agg_read")
        dense_ready = sem("dense_ready")
        act_done = sem("act_done")
        leaky_done = sem("leaky_done")
        out_stored = sem("out_stored")

        block = ctx.enter_context(nc.Block())

        N_ADJ = 3
        TB = [(0, 4), (4, 4), (8, T - 8)]

        @block.sync
        def _(sp):
            sp.dma_start(w_nat[:, 0, :, :], wqkv[0].rearrange("(j h) c -> j h c", h=H)).then_inc(w_loaded[0], 16)
            sp.dma_start(x_nat[:, 0:T - 1, :], x[0:(T - 1) * P, :].rearrange("(i p) d -> p i d", p=P)).then_inc(x_loaded, 16)
            sp.dma_start(x_nat[0:RP[-1], T - 1, :], x[(T - 1) * P:N, :]).then_inc(x_loaded, 16)
            for w in (1, 2):
                sp.dma_start(w_nat[:, w, :, :], wqkv[w].rearrange("(j h) c -> j h c", h=H)).then_inc(w_loaded[w], 16)
            def load_adj(i):
                if i == 0:
                    sp.wait_ge(wt_ready, 9)
                    sp.wait_ge(wt_read, 9)
                    sp.dma_start(x_cols, xT0[:, 0:N]).then_inc(xt_stored, 16)
                if i >= 2:
                    sp.wait_ge(adjt_ready, N_ADJ * (i - 1))
                    sp.wait_ge(bmax_ready, i - 1)
                sp.dma_start(adj_nat[i % 2][0:RP[i], 0:N], adj[P * i:P * i + RP[i], :]).then_inc(adj_loaded[i % 2], 16)

            for i in range(2):
                load_adj(i)
            for i in range(T):
                r = RP[i]
                for w in range(2):
                    e = 2 * i + w
                    sp.wait_ge(part3_ready, e + 1)
                    for k in range(PARTS):
                        sp.dma_start(qk_parts[w, k, :, P * P * i:P * P * i + r * P].rearrange("h (r j) -> r h j", j=P),
                                     parts[e % SPLITS][0:r, k, :].rearrange("p (h j) -> p h j", h=H)).then_inc(parts_stored[e % SPLITS], 16)
                sp.wait_ge(proj_read, 3 * i + 3)
                sp.dma_start(v_rows[P * P * V1 * i:P * V1 * (P * i + r)].rearrange("(r j) -> r j", j=P * V1),
                             v_out[i % 2][0:r, :, :].rearrange("p j h -> p (j h)")).then_inc(v_stored[i % 2], 16)
                if i + 2 < T:
                    load_adj(i + 2)
            for i in range(SPLITS):
                sp.wait_ge(parts_stored[i], 48 * len(range(i, 2 * T, SPLITS)))
            for i in range(2):
                sp.wait_ge(v_stored[i], 16 * len(range(i, T, 2)))

            def load_qk(g, par):
                for b in range(PARTS):
                    sp.dma_start(q_sb[24 * b:24 * b + 24, par, :, 0:N],
                                 qk_parts[0].rearrange("k h g -> (k h) g")[:, bass.ds(g * (HG * N), HG * N)]
                                 .rearrange("r (a n) -> r a n", a=HG)).then_inc(qk_loaded[par], 16)
                    for a in range(PARTS):
                        sp.dma_start(k_sb[24 * b + 8 * a:24 * b + 8 * a + 8, par, :, :].rearrange("r a n -> r (a n)"),
                                     qk_parts[1, b, :, bass.ds(g * (HG * N), HG * N)]).then_inc(qk_loaded[par], 16)

            def load_v(g, par):
                src = v_rows[bass.ds(g * (HG * N * V1), HG * N * V1)].rearrange("(a m) -> a m", a=HG)
                full = (KROWS - 1) * T * V1
                sp.dma_start(v_sb[0:KROWS - 1, par, :, :],
                             src[:, 0:full].rearrange("a (p x) -> p a x", x=T * V1)).then_inc(v_loaded[par], 16)
                sp.dma_start(v_sb[KROWS - 1:KROWS, par, :, 0:V1], src[:, full:full + V1].rearrange("(o a) x -> o a x", o=1)).then_inc(v_loaded[par], 16)

            def maxrows(it, beta):
                gbase, b = divmod(beta, len(BATCHES))
                i0, n = BATCHES[b]
                sp.wait_ge(split_step, it * (6 * len(BATCHES)) + (3 * beta + 3))
                sp.dma_start(max_rows[b].rearrange("k x j -> x k j"), rowparts[0:HG * n, b, :, :]).then_inc(maxrow_stored, 16)
                sp.wait_ge(maxrow_stored, it * (32 * len(BATCHES)) + 16 * (beta + 1))
                sp.dma_start(q_sb[ZROWS:MAXROWS, gbase % 2, :, P * i0:P * (i0 + n)],
                             max_rows[b].rearrange("k (a i) j -> k a (i j)", a=HG)).then_inc(maxrow_loaded[b], 16)

            def store(g, q, c, cnt):
                sp.wait_ge(o_copied, cnt + 1)
                for a in range(HG):
                    sp.dma_start(att[:, bass.ds(g * (HG * N) + (a * N + C0[c]), CW[c])],
                                 o_sb[32 * a:32 * a + V1, q % 2, 0:CW[c]]).then_inc(o_stored[q % 2], 16)

            sp.wait_ge(spare_rows, 5)
            load_qk(0, 0)
            load_v(0, 0)
            sp.wait_ge(brow_step, 4)
            for k in range(PARTS):
                sp.dma_start(biasrow[k:k + 1, :].rearrange("o (i j) -> o i j", j=P), rowparts[0:T, 0, k, :]).then_inc(brow_copied, 16)
            sp.wait_ge(brow_copied, 16 * PARTS)
            sp.dma_start(q_sb[MAXROWS:ALLROWS, :, :, :].rearrange("k g a n -> k (g a) n"),
                         biasrow[:].unsqueeze(1).to_broadcast([PARTS, 2 * HG, NPAD])).then_inc(brow_spread, 16)
            sp.wait_ge(brow_spread, 16)
            load_qk(1, 1)
            maxrows(0, 0)
            load_v(1, 1)

            def group(it, par, more_qk, more_max):
                g = it * 2 + par
                for c in range(NC - 1):
                    maxrows(it, 3 * par + c + 1)
                    store(g, NC * par + c, c, it * (2 * NC) + (NC * par + c + 1))
                if more_max:
                    maxrows(it, 3 * par + 3)
                if more_qk:
                    sp.wait_ge(st_ready, it * (2 * HG * STEPS) + HG * STEPS * (par + 1))
                    load_qk(g + 2, par)
                store(g, NC * par + 2, 2, it * (2 * NC) + (NC * par + 3))
                if more_qk:
                    sp.wait_ge(pv_done, it * (2 * STEPS) + STEPS * (par + 1))
                    load_v(g + 2, par)

            with sp.Fori(0, NG // 2 - 1) as it:
                group(it, 0, True, True)
                group(it, 1, True, True)
            group(NG // 2 - 1, 0, False, True)
            group(NG // 2 - 1, 1, False, False)
            for i in range(2):
                sp.wait_ge(o_stored[i], 64 * (NG // 2) * NC + 16)
            sp.wait_ge(xt_stored, 16)
            sp.dma_start(wo_nat, wo).then_inc(wo_loaded, 16)
            for i in range(T):
                if i >= 3:
                    sp.wait_ge(ot_ready, 2 * (i - 2))
                sp.dma_start(o_nat[i % 3][0:RP[i], :, :],
                             att[:, P * P * i:P * P * i + P * RP[i]].rearrange("h (r j) -> r h j", j=P)).then_inc(on_loaded[i % 3], 16)
            sp.dma_start(xT[:, 0:N], x_cols).then_inc(xt_loaded, 16)
            for n in range(8):
                sp.dma_start(wts[:, n, :], weights[n]).then_inc(small_loaded, 16)
                sp.dma_start(bia[:, n:n + 1], biases[n].rearrange("(d o) -> d o", o=1)).then_inc(small_loaded, 16)
            sp.wait_ge(nat_read, NC * (len(PROPS) + 1))
            full = (KROWS - 1) * T
            sp.dma_start(out[0:full, :].rearrange("(p t) d -> p t d", t=T), nat[0:KROWS - 1, :, :]).then_inc(out_stored, 16)
            sp.dma_start(out[full:N, :], nat[KROWS - 1:KROWS, 0, :]).then_inc(out_stored, 16)
            sp.wait_ge(out_stored, 32)

        @block.gpsimd
        def _(pool):
            nc.gpsimd.memset(ident[:], 0.0).then_inc(s_ident, 1)
            pool.wait_ge(s_ident, 1)
            nc.gpsimd.affine_select(out=ident[:], in_=ident[:], compare_op=ALU.not_equal, fill=1.0, base=0,
                                    pattern=[[-1, P]], channel_multiplier=1).then_inc(s_ident, 1)
            fills = [(q_sb[0:64, :, :, N:NPAD], 0.0), (q_sb[64:96, :, :, :], 0.0), (k_sb[64:96, :, :, :], 0.0),
                     (k_sb[96:128, :, :, :], 1.0), (v_sb[:], 0.0)]
            for n, (dst, value) in enumerate(fills):
                if n:
                    pool.wait_ge(spare_rows, n)
                nc.gpsimd.memset(dst, value).then_inc(spare_rows, 1)
            pool.wait_ge(eb_ready, MULS)

            def mults(it, u):
                c, t = divmod(u % STEPS, T)
                pool.wait_ge(exps_done, it * (2 * HG * EXPS) + HG * (exps_before(u) + 1))
                w = ring[0:NKEYS[t], slot(u), :, 0:CW[c]]
                e = ebias[0:NKEYS[t], muls_before(u % STEPS), 0:CW[c]].unsqueeze(1).to_broadcast([NKEYS[t], HG, CW[c]])
                nc.gpsimd.tensor_tensor(w, w, e, ALU.mult).then_inc(mults_done, 1)

            with pool.Fori(0, NG // 2) as it:
                for u in range(2 * STEPS):
                    if kind(u) == MUL:
                        mults(it, u)

        @block.scalar
        def _(act):
            for b in range(9):
                act.wait_ge(wt_ready, b + 1)
                if b < 3:
                    a = 512 * b
                    w = min(512, N - a)
                    nc.scalar.activation(xT0[:, a:a + w], ps[:, b % 8, 0:w], ACT.Copy).then_inc(wt_read, 1)
                else:
                    dst = wT[:, (b - 3) // 2, 512 * ((b - 3) % 2):512 * ((b - 3) % 2) + 512]
                    nc.scalar.activation(dst, ps[:, b % 8, :], ACT.Copy).then_inc(wt_read, 1)
            def second(e):
                r = RP[e // 2]
                act.wait_ge(rem1_ready, e + 1)
                nc.scalar.activation(parts[e % SPLITS][0:r, 1, :], rem[e % SPLITS][0:r, :], ACT.Copy).then_inc(part2_ready, 1)

            for i in range(T):
                r = RP[i]
                for w in range(3):
                    s = 3 * i + w
                    src = ps[0:r, 2 * (s % 2):2 * (s % 2) + 2, :].rearrange("p b n -> p (b n)")
                    act.wait_ge(proj_ready, s + 1)
                    if w < 2:
                        e = 2 * i + w
                        sc = SCALE if w == 0 else 1.0
                        if e >= SPLITS:
                            act.wait_ge(part3_ready, e - SPLITS + 1)
                            act.wait_ge(parts_stored[e % SPLITS], 48 * (e // SPLITS))
                        nc.scalar.activation(rem[e % SPLITS][0:r, :], src, ACT.Copy, scale=sc)
                        nc.scalar.activation(parts[e % SPLITS][0:r, 0, :], src, ACT.Copy, scale=sc).then_inc(proj_read, 1)
                        if e:
                            second(e - 1)
                    else:
                        if i == 0:
                            act.wait_ge(fill, 1)
                        if i >= 2:
                            act.wait_ge(v_stored[i % 2], 16 * (i // 2))
                        nc.scalar.activation(v_out[i % 2][0:r, :, 0:H].rearrange("p j h -> p h j"),
                                             src.rearrange("p (h j) -> p h j", h=H), ACT.Copy).then_inc(proj_read, 1)
                for b, (t0, nt) in enumerate(TB):
                    n = N_ADJ * i + b
                    act.wait_ge(adjt_ready, n + 1)
                    nc.scalar.activation(adjT[0:KROWS, t0:t0 + nt, P * i:P * i + RP[i]],
                                         ps[0:KROWS, 4 + n % 3, :].rearrange("p (t n) -> p t n", n=P)[:, 0:nt, 0:RP[i]],
                                         ACT.Copy).then_inc(adjt_read, 1)
            second(2 * T - 1)
            for m in range(MULS):
                act.wait_ge(eb_sum, m + 1)
                s = [s for s in range(STEPS) if kind(s) == MUL][m]
                e = ebias[0:NKEYS[s % T], m, 0:CW[s // T]]
                nc.scalar.activation(e, e, ACT.Exp).then_inc(eb_ready, 1)

            def exps(it, u):
                c, t = divmod(u % STEPS, T)

                if kind(u) == ADD:
                    return
                if last_user(u) >= 0 or not isinstance(it, int) or it > 0:
                    act.wait_ge(pv_done, it * (2 * STEPS) + (last_user(u) + 1))
                for a in range(HG):
                    j = HG * u + a
                    act.wait_ge(st_ready, it * (2 * HG * STEPS) + (j + 1))
                    nc.scalar.activation(ring[0:NKEYS[t], slot(u), a, 0:CW[c]], ps[0:NKEYS[t], ST_BANK + j % 3, 0:CW[c]],
                                         ACT.Exp).then_inc(exps_done, 1)

            def sbexps(it, u):
                if kind(u) != ADD:
                    return
                c, t = divmod(u % STEPS, T)
                act.wait_ge(adds_done, it * (2 * HG * ADDS) + HG * (adds_before(u) + 1))
                w = ring[0:NKEYS[t], slot(u), :, 0:CW[c]]
                nc.scalar.activation(w, w, ACT.Exp).then_inc(sbexp_done, 1)

            def copy_sums(it, q):
                act.wait_ge(pv_done, it * (2 * STEPS) + T * (q + 1))
                act.wait_ge(o_stored[q % 2], it * (64 * NC) + (64 * (q // 2) + 16))
                nc.scalar.activation(o_sb[0:96 + V1, q % 2, 0:CW[q % NC]], ps[0:96 + V1, PV_BANK, 0:CW[q % NC]],
                                     ACT.Copy).then_inc(o_copied, 1)

            for u in range(ACT_LEAD):
                exps(0, u)
                if u:
                    sbexps(0, u - 1)

            def body(it, last):
                for xx in range(2 * STEPS):
                    u = xx + ACT_LEAD
                    if xx % T == T - 1:
                        copy_sums(it, xx // T)
                    if u < 2 * STEPS or not last:
                        exps(it, u)
                    if u - 1 < 2 * STEPS or not last:
                        sbexps(it, u - 1)

            with act.Fori(0, NG // 2 - 1) as it:
                body(it, False)
            body(NG // 2 - 1, True)

            for b in range(2):
                act.wait_ge(wot_ready, b + 1)
                nc.scalar.activation(woT[:, 4 * b:4 * b + 4, :].rearrange("p h d -> p (h d)"), ps[:, 6 + b, :],
                                     ACT.Copy).then_inc(wot_read, 1)
            for i in range(T):
                for b in range(2):
                    n = 2 * i + b
                    act.wait_ge(ot_ready, n + 1)
                    nc.scalar.activation(oT[:, 4 * b:4 * b + 4, P * i:P * i + RP[i]],
                                         ps[:, n % 6, :].rearrange("p (h n) -> p h n", n=P)[:, :, 0:RP[i]],
                                         ACT.Copy).then_inc(ot_read, 1)

            def norm(k):
                def std(c):
                    act.wait_ge(var_ready, NC * k + c + 1)
                    nc.scalar.activation(sq[:, C0[c]:C0[c] + CW[c]], ps[:, 7, 0:CW[c]], ACT.Sqrt, bias=epst[:]).then_inc(std_ready, 1)

                for c in range(NC):
                    act.wait_ge(cen_ready, NC * k + c + 1)
                    cs = slice(C0[c], C0[c] + CW[c])
                    nc.scalar.activation(sq[:, cs], cen[:, cs], ACT.Square).then_inc(sq_ready, 1)
                    if c:
                        std(c - 1)
                std(NC - 1)

            def naturals(k, rows):
                for b, (t0, nt) in enumerate(TB):
                    n = NC * k + b
                    act.wait_ge(nat_ready, n + 1)
                    nc.scalar.activation(nat[0:KROWS, t0:t0 + nt, :],
                                         ps[0:KROWS, 5 + b, 0:nt * D].rearrange("p (t d) -> p t d", d=D),
                                         ACT.Copy).then_inc(nat_read, 1)

            norm(0)
            dense = 0
            for k, (src, layers, fn) in enumerate(PROPS):
                naturals(k, None)
                for st, c in wave(len(layers)):
                    cs = slice(C0[c], C0[c] + CW[c])
                    if st == 0:
                        act.wait_ge(agg_ready, NC * k + c + 1)
                        nc.scalar.activation(z_sb[:, cs], ps[:, c, 0:CW[c]], ACT.Copy).then_inc(agg_read, 1)
                        continue
                    act.wait_ge(dense_ready, dense + 1)
                    src_ps = ps[:, 3 + dense % 2, 0:CW[c]]
                    b = bia[:, layers[st - 1]:layers[st - 1] + 1]
                    if fn == "leaky":
                        nc.scalar.activation(leak[:, cs], src_ps, ACT.Identity, bias=b).then_inc(act_done, 1)
                    else:
                        nc.scalar.activation(out_sb[:, cs], src_ps, ACT.Silu if fn == "silu" else ACT.Relu, bias=b).then_inc(act_done, 1)
                    dense += 1
                if k in NORM_AFTER:
                    norm(NORM_AFTER[k])
            naturals(len(PROPS), None)

        @block.vector
        def _(dve):
            def third(e):
                r = RP[e // 2]
                dve.wait_ge(part2_ready, e + 1)
                nc.vector.tensor_tensor(parts[e % SPLITS][0:r, 2, :], rem[e % SPLITS][0:r, :], parts[e % SPLITS][0:r, 1, :],
                                        ALU.subtract).then_inc(part3_ready, 1)

            nc.vector.memset(v_out[0][:, :, H:V1], 1.0)
            nc.vector.memset(v_out[1][:, :, H:V1], 1.0)
            nc.vector.memset(avg[:], 1.0 / D)
            nc.vector.memset(epst[:], EPS)
            nc.vector.memset(ones3[:], 1.0).then_inc(fill, 1)
            for i in range(2):
                nc.vector.memset(o_sb[:, i, :], 0.0).then_inc(o_stored[i], 16)
            for b in range(len(BATCHES)):
                nc.vector.memset(rowparts[:, b, :, :], 0.0).then_inc(maxrow_loaded[b], 16)
            dve.wait_ge(wt_ready, 9)
            for i in range(2):
                nc.vector.memset(adj_nat[i][:, N:NPAD], 0.0).then_inc(fill, 1)
            dve.wait_ge(s_ident, 2)
            nc.vector.tensor_scalar(ident2[:], ident[:], 2.0, None, ALU.mult).then_inc(fill, 1)
            nc.vector.memset(negmax[:], 0.0).then_inc(pv_clear, 1)
            dve.wait_ge(pv_clear, 1)
            for e in range(2 * T):
                i, w = divmod(e, 2)
                r = RP[i]
                dve.wait_ge(proj_read, 3 * i + w + 1)
                nc.vector.tensor_tensor(rem[e % SPLITS][0:r, :], rem[e % SPLITS][0:r, :], parts[e % SPLITS][0:r, 0, :],
                                        ALU.subtract).then_inc(rem1_ready, 1)
                if e:
                    third(e - 1)
                if w == 1:
                    dve.wait_ge(adj_loaded[i % 2], 16 * (i // 2 + 1))
                    nc.vector.tensor_reduce(negmax[0:RP[i], i:i + 1], adj_nat[i % 2][0:RP[i], 0:N], op=ALU.max,
                                            axis=AX.X, negate=True).then_inc(bmax_ready, 1)
            third(2 * T - 1)
            dve.wait_ge(brow_ready, 1)
            nc.vector.tensor_scalar(rowparts[0:T, 0, 0, :], ps[0:T, 7, 0:P], 2.0, None, ALU.mult).then_inc(brow_step, 1)
            dve.wait_ge(brow_step, 1)
            nc.vector.scalar_tensor_tensor(out=rowrem[0:T, :], in0=ps[0:T, 7, 0:P], scalar=2.0, in1=rowparts[0:T, 0, 0, :],
                                           op0=ALU.mult, op1=ALU.subtract).then_inc(brow_step, 1)
            dve.wait_ge(brow_step, 2)
            nc.vector.tensor_copy(rowparts[0:T, 0, 1, :], rowrem[0:T, :]).then_inc(brow_step, 1)
            dve.wait_ge(brow_step, 3)
            nc.vector.tensor_tensor(rowparts[0:T, 0, 2, :], rowrem[0:T, :], rowparts[0:T, 0, 1, :], ALU.subtract).then_inc(brow_step, 1)
            def max_pair(it, z, p):
                sl = slot_of(z) + p
                col = 2 * (PAIR_FROM[z % STEPS] + p)
                dve.wait_ge(s_ready, it * (2 * SLOTS) + (sl + 1))
                nc.vector.tensor_reduce(maxes[:, col:col + 2], ps[:, 2 * (sl % 2):2 * (sl % 2) + 2, 0:MW], op=ALU.max,
                                        axis=AX.X).then_inc(s_read, 1)

            def batch_max(it, z):
                beta = batch_before(z + 1)
                if beta is None:
                    return
                i0, n = BATCHES[beta % 3]
                dve.wait_ge(s_read, it * (2 * SLOTS) + (slot_of(z) + PASS_PAIRS[z % STEPS]))
                nc.vector.tensor_reduce(negmax[:, 0:HG * n].rearrange("p (a i) -> p i a", i=n),
                                        maxes[:, HG * NC * i0:HG * NC * (i0 + n)].rearrange("p (i a c) -> p i a c", a=HG, c=NC),
                                        op=ALU.max, axis=AX.X, negate=True).then_inc(negmax_ready, 1)

            def split_max(it, z, sl):
                beta = batch_before(z)
                gbase, b = divmod(beta, len(BATCHES))
                n = HG * BATCHES[b][1]
                src = ps[0:n, 2 * (sl % 2), 0:P]
                dve.wait_ge(s_ready, it * (2 * SLOTS) + (sl + 1))
                if isinstance(it, int) and it == 0 and beta == 0:
                    dve.wait_ge(brow_copied, 16 * PARTS)
                dve.wait_ge(maxrow_loaded[b], it * 32 + (16 * gbase + 16))
                nc.vector.tensor_copy(rowparts[0:n, b, 0, :], src).then_inc(split_step, 1)
                dve.wait_ge(split_step, it * (6 * len(BATCHES)) + (3 * beta + 1))
                nc.vector.tensor_tensor(rowrem[0:n, :], src, rowparts[0:n, b, 0, :], ALU.subtract).then_inc(s_read, 1)
                dve.wait_ge(s_read, it * (2 * SLOTS) + (sl + 1))
                nc.vector.tensor_copy(rowparts[0:n, b, 1, :], rowrem[0:n, :]).then_inc(split_step, 1)
                dve.wait_ge(split_step, it * (6 * len(BATCHES)) + (3 * beta + 2))
                nc.vector.tensor_tensor(rowparts[0:n, b, 2, :], rowrem[0:n, :], rowparts[0:n, b, 1, :],
                                        ALU.subtract).then_inc(split_step, 1)

            def add_bias(it, u, a):
                c, t = divmod(u % STEPS, T)
                if a == 0 and (last_user(u) >= 0 or not isinstance(it, int) or it > 0):
                    dve.wait_ge(pv_done, it * (2 * STEPS) + (last_user(u) + 1))
                j = HG * u + a
                dve.wait_ge(st_ready, it * (2 * HG * STEPS) + (j + 1))
                nc.vector.scalar_tensor_tensor(
                    out=ring[0:NKEYS[t], slot(u), a, 0:CW[c]], in0=adjT[0:NKEYS[t], t, C0[c]:C0[c] + CW[c]],
                    scalar=2.0, in1=ps[0:NKEYS[t], ST_BANK + j % 3, 0:CW[c]], op0=ALU.mult,
                    op1=ALU.add).then_inc(adds_done, 1)

            def step(it, u, maxing, scoring=True):
                z = u + AHEAD
                for x in plan(u, maxing) if scoring else [p + 10 for p in range(PASS_PAIRS[z % STEPS])]:
                    if not isinstance(x, str):
                        max_pair(it, z, x - 10)
                    elif x != "V" and kind(u) == ADD:
                        add_bias(it, u, int(x))
                if maxing:
                    batch_max(it, z)
                if batch_before(z) is not None and (maxing or z == 2 * STEPS):
                    split_max(it, z, slot_of(z) + (PASS_PAIRS[z % STEPS] if maxing else 0))

            for u in range(-AHEAD, 0):
                step(0, u, True, False)
            dve.wait_ge(v_stored[1], 16 * len(range(1, T, 2)))
            dve.wait_ge(adjt_read, N_ADJ * T)
            for m, s in enumerate(s for s in range(STEPS) if kind(s) == MUL):
                c, t = divmod(s, T)
                dve.wait_ge(bb_ready, c + 1)
                nc.vector.scalar_tensor_tensor(out=ebias[0:NKEYS[t], m, 0:CW[c]], in0=adjT[0:NKEYS[t], t, C0[c]:C0[c] + CW[c]],
                                               scalar=2.0, in1=ps[0:NKEYS[t], ST_BANK + c, 0:CW[c]], op0=ALU.mult,
                                               op1=ALU.add).then_inc(eb_sum, 1)
            nc.vector.memset(ps[:, PV_BANK, :], 0.0).then_inc(o_copied, 1)

            for u in range(DVE_LEAD):
                step(0, u, True)
            with dve.Fori(0, NG // 2 - 1) as it:
                for xx in range(2 * STEPS):
                    step(it, xx + DVE_LEAD, True)
            for u in range(DVE_LEAD, 2 * STEPS):
                step(NG // 2 - 1, u, u + AHEAD < 2 * STEPS)

            for i in range(T):
                r = RP[i]
                dve.wait_ge(on_loaded[i % 3], 16 * (i // 3 + 1))
                o = o_nat[i % 3]
                if i >= 2:
                    dve.wait_ge(on_ready, i - 1)
                nc.vector.reciprocal(rsum[i % 2][0:r, :], o[0:r, H, :]).then_inc(rsum_ready, 1)
                dve.wait_ge(rsum_ready, i + 1)
                nc.vector.tensor_tensor(o[0:r, 0:H, :], o[0:r, 0:H, :], rsum[i % 2][0:r, :].unsqueeze(1).to_broadcast([r, H, P]),
                                        ALU.mult).then_inc(on_ready, 1)

            def norm(k, layer_chunk):
                def close(c):
                    cs = slice(C0[c], C0[c] + CW[c])
                    dve.wait_ge(std_ready, NC * k + c + 1)
                    nc.vector.reciprocal(sq[:, cs], sq[:, cs]).then_inc(inv_ready, 1)
                    dve.wait_ge(inv_ready, NC * k + c + 1)
                    nc.vector.tensor_tensor(xT[:, cs], cen[:, cs], sq[:, cs], ALU.mult).then_inc(x_ready, 1)

                for c in range(NC):
                    cs = slice(C0[c], C0[c] + CW[c])
                    y = layer_chunk(c)
                    nc.vector.tensor_tensor(z_sb[:, cs], y, xT[:, cs], ALU.add).then_inc(z_ready, 1)
                for c in range(NC):
                    cs = slice(C0[c], C0[c] + CW[c])
                    dve.wait_ge(mean_ready, NC * k + c + 1)
                    nc.vector.tensor_tensor(cen[:, cs], z_sb[:, cs], ps[:, 5 + c % 2, 0:CW[c]], ALU.subtract).then_inc(cen_ready, 1)
                for c in range(NC):
                    close(c)

            def projected(c):
                dve.wait_ge(y_ready, c + 1)
                return ps[:, 6 + c % 2, 0:CW[c]] if c < 2 else ps[:, 0, 0:CW[c]]

            dve.wait_ge(y_ready, 1)
            dve.wait_ge(xt_loaded, 16)
            nc.vector.memset(out_sb[:, N:NPAD], 0.0)
            nc.vector.memset(xT[:, N:NPAD], 0.0)
            norm(0, projected)
            dense = 0
            lk = 0
            for k, (src, layers, fn) in enumerate(PROPS):
                for st, c in wave(len(layers)):
                    if st == 0:
                        continue
                    dense += 1
                    if fn == "leaky":
                        cs = slice(C0[c], C0[c] + CW[c])
                        dst = out_sb if st == len(layers) else mid[st - 1]
                        dve.wait_ge(act_done, dense)
                        nc.vector.scalar_tensor_tensor(out=dst[:, cs], in0=leak[:, cs], scalar=0.01, in1=leak[:, cs],
                                                       op0=ALU.mult, op1=ALU.max).then_inc(leaky_done, 1)
                        lk += 1
                if k in NORM_AFTER:
                    if fn == "leaky":
                        dve.wait_ge(leaky_done, lk)
                    dve.wait_ge(act_done, dense)
                    norm(NORM_AFTER[k], lambda c: out_sb[:, C0[c]:C0[c] + CW[c]])

        @block.tensor
        def _(pe):
            pe.wait_ge(s_ident, 2)
            for b in range(9):
                if b == 0:
                    pe.wait_ge(x_loaded, 32)
                elif b % 2 == 1 and b >= 3:
                    pe.wait_ge(w_loaded[(b - 3) // 2], 16)
                if b >= 8:
                    pe.wait_ge(wt_read, b - 7)
                for q in range(4):
                    if b >= 3:
                        src = w_nat[:, (b - 3) // 2, 4 * ((b - 3) % 2) + q, :]
                    elif 4 * b + q < T:
                        src = x_nat[0:RP[4 * b + q], 4 * b + q, :]
                    else:
                        continue
                    r = src.shape[0]
                    last = nc.tensor.transpose(ps[:, b % 8, P * q:P * q + r], src, ident[0:r, 0:r])
                last.then_inc(wt_ready, 1)
            pe.wait_ge(wt_read, 9)
            for i in range(T):
                for w in range(3):
                    s = 3 * i + w
                    if s >= 2:
                        pe.wait_ge(proj_read, s - 1)
                    for h in range(2):
                        last = nc.tensor.matmul(ps[0:RP[i], 2 * (s % 2) + h, :], xT0[:, P * i:P * i + RP[i]],
                                                wT[:, w, 512 * h:512 * h + 512], start=True, stop=True)
                    last.then_inc(proj_ready, 1)
                pe.wait_ge(adj_loaded[i % 2], 16 * (i // 2 + 1))
                if i == 0:
                    pe.wait_ge(fill, 4)
                cols = adj_nat[i % 2][0:RP[i], 0:T * KROWS].rearrange("p (m t) -> p t m", t=T)
                for b, (t0, nt) in enumerate(TB):
                    n = N_ADJ * i + b
                    if n >= 3:
                        pe.wait_ge(adjt_read, n - 2)
                    for t in range(t0, t0 + nt):
                        last = nc.tensor.transpose(ps[0:KROWS, 4 + n % 3, P * (t - t0):P * (t - t0) + RP[i]], cols[:, t, :],
                                                   ident[0:RP[i], 0:RP[i]])
                    last.then_inc(adjt_ready, 1)
            pe.wait_ge(bmax_ready, T)
            nc.tensor.transpose(ps[:, 7, 0:P], negmax[:], ident[:]).then_inc(brow_ready, 1)
            def score_pair(it, z, p):
                gbase, w = divmod(z, STEPS)
                par = gbase % 2
                sl = slot_of(z) + p
                if not (isinstance(it, int) and it == 0 and sl < 2):
                    pe.wait_ge(s_read, it * (2 * SLOTS) + (sl - 1))
                if PAIR_FROM[w] + p == 0:
                    pe.wait_ge(qk_loaded[par], it * 192 + 192 * (gbase // 2 + 1))
                for e in range(2):
                    i, rest = divmod(2 * (PAIR_FROM[w] + p) + e, HG * NC)
                    a, c = divmod(rest, NC)
                    last = nc.tensor.matmul(ps[:, 2 * (sl % 2) + e, 0:MW], q_sb[0:ZROWS, par, a, P * i:P * i + P],
                                            k_sb[0:ZROWS, par, a, M0[c]:M0[c] + MW], start=True, stop=True)
                last.then_inc(s_ready, 1)

            def turn_max(it, z, sl):
                pe.wait_ge(s_read, it * (2 * SLOTS) + (sl - 1))
                pe.wait_ge(negmax_ready, it * (2 * len(BATCHES)) + (batch_before(z) + 1))
                nc.tensor.transpose(ps[:, 2 * (sl % 2), 0:P], negmax[:], ident[:]).then_inc(s_ready, 1)

            def scores(it, u, a):
                s = u % STEPS
                par = u // STEPS % 2
                c, t = divmod(s, T)
                rows = MAXROWS if kind(u) == MUL else ALLROWS
                if t == 0 and a == 0:
                    pe.wait_ge(maxrow_loaded[c], it * 32 + (16 * (u // STEPS + 1) + 16))
                j = HG * u + a
                jb = j - 3
                if jb >= 0 or not isinstance(it, int) or it > 0:
                    ub = jb // HG
                    if kind(ub) != ADD:
                        pe.wait_ge(exps_done, it * (2 * HG * EXPS) + (HG * exps_before(ub) + jb % HG + 1))
                    else:
                        pe.wait_ge(adds_done, it * (2 * HG * ADDS) + (HG * adds_before(ub) + jb % HG + 1))
                bank = ps[0:NKEYS[t], ST_BANK + j % 3, 0:CW[c]]
                last = nc.tensor.matmul(bank, k_sb[0:rows, par, a, t:t + T * (NKEYS[t] - 1) + 1:T],
                                        q_sb[0:rows, par, a, C0[c]:C0[c] + CW[c]], start=True, stop=kind(u) != PE)
                if kind(u) == PE:
                    last = nc.tensor.matmul(bank, ident2[0:NKEYS[t], 0:NKEYS[t]], adjT[0:NKEYS[t], t, C0[c]:C0[c] + CW[c]],
                                            start=False, stop=True)
                last.then_inc(st_ready, 1)

            def values(it, u):
                s = u % STEPS
                par = u // STEPS % 2
                c, t = divmod(s, T)
                if kind(u) == MUL:
                    pe.wait_ge(mults_done, it * (2 * MULS) + (muls_before(u) + 1))
                elif kind(u) == PE:
                    pe.wait_ge(exps_done, it * (2 * HG * EXPS) + HG * (exps_before(u) + 1))
                else:
                    pe.wait_ge(sbexp_done, it * (2 * ADDS) + (adds_before(u) + 1))
                if s == 0:
                    pe.wait_ge(v_loaded[par], it * 32 + 32)
                if t == 0:
                    pe.wait_ge(o_copied, it * (2 * NC) + (u // T + 1))
                r = NKEYS[t]
                for a in range(HG):
                    last = nc.tensor.matmul(ps[32 * a:32 * a + V1, PV_BANK, 0:CW[c]], v_sb[0:r, par, a, V1 * t:V1 * t + V1],
                                            ring[0:r, slot(u), a, 0:CW[c]], start=(t == 0), stop=(t == T - 1))
                last.then_inc(pv_done, 1)

            def step(it, u, maxing, scoring, with_values):
                z = u + AHEAD
                for x in plan(u, maxing):
                    if not isinstance(x, str):
                        score_pair(it, z, x - 10)
                    elif x == "V":
                        if with_values:
                            values(it, u - LAG)
                    elif scoring:
                        scores(it, u, int(x))
                if batch_before(z) is not None and (maxing or z == 2 * STEPS):
                    turn_max(it, z, slot_of(z) + (PASS_PAIRS[z % STEPS] if maxing else 0))

            for u in range(-AHEAD, 0):
                step(0, u, True, False, False)
            pe.wait_ge(brow_copied, 16 * PARTS)
            pe.wait_ge(adjt_read, N_ADJ * T)
            for c in range(NC):
                nc.tensor.matmul(ps[0:KROWS, ST_BANK + c, 0:CW[c]], ones3[:], biasrow[:, C0[c]:C0[c] + CW[c]], start=True,
                                 stop=True).then_inc(bb_ready, 1)
            pe.wait_ge(eb_sum, MULS)
            for u in range(LAG):
                step(0, u, True, True, False)
            with pe.Fori(0, NG // 2 - 1) as it:
                for xx in range(2 * STEPS):
                    step(it, xx + LAG, True, True, True)
            for u in range(LAG, 2 * STEPS + LAG):
                step(NG // 2 - 1, u, u + AHEAD < 2 * STEPS, u < 2 * STEPS, True)

            pe.wait_ge(wo_loaded, 16)
            pe.wait_ge(o_copied, NC * NG + 1)
            for b in range(2):
                for h in range(4):
                    last = nc.tensor.transpose(ps[:, 6 + b, P * h:P * h + P],
                                               wo_nat.rearrange("p (j h) -> p h j", h=H)[:, 4 * b + h, :], ident[:])
                last.then_inc(wot_ready, 1)
            for i in range(T):
                pe.wait_ge(on_ready, i + 1)
                for b in range(2):
                    n = 2 * i + b
                    if n >= 6:
                        pe.wait_ge(ot_read, n - 5)
                    for h in range(4):
                        last = nc.tensor.transpose(ps[:, n % 6, P * h:P * h + RP[i]], o_nat[i % 3][0:RP[i], 4 * b + h, :],
                                                   ident[0:RP[i], 0:RP[i]])
                    last.then_inc(ot_ready, 1)
            pe.wait_ge(ot_read, 2 * T)
            pe.wait_ge(wot_read, 2)
            for c in range(NC):
                dst = ps[:, 6 + c % 2, 0:CW[c]] if c < 2 else ps[:, 0, 0:CW[c]]
                for h in range(H):
                    last = nc.tensor.matmul(dst, woT[:, h, :], oT[:, h, C0[c]:C0[c] + CW[c]], start=(h == 0), stop=(h == H - 1))
                last.then_inc(y_ready, 1)

            def norm(k):
                def var(c):
                    pe.wait_ge(sq_ready, NC * k + c + 1)
                    if c:
                        pe.wait_ge(std_ready, NC * k + c)
                    nc.tensor.matmul(ps[:, 7, 0:CW[c]], avg[:], sq[:, C0[c]:C0[c] + CW[c]], start=True, stop=True).then_inc(var_ready, 1)

                pe.wait_ge(z_ready, NC * k + NC)
                for c in range(NC):
                    if c == 2:
                        pe.wait_ge(cen_ready, NC * k + 1)
                    nc.tensor.matmul(ps[:, 5 + c % 2, 0:CW[c]], avg[:], z_sb[:, C0[c]:C0[c] + CW[c]], start=True, stop=True).then_inc(mean_ready, 1)
                    if c:
                        var(c - 1)
                var(NC - 1)

            def naturals(k, src):
                cols = src[:, 0:T * KROWS].rearrange("p (m t) -> p t m", t=T)
                for b, (t0, nt) in enumerate(TB):
                    for t in range(t0, t0 + nt):
                        last = nc.tensor.transpose(ps[0:KROWS, 5 + b, P * (t - t0):P * (t - t0) + D], cols[:, t, :], ident[:])
                    last.then_inc(nat_ready, 1)

            pe.wait_ge(small_loaded, 256)
            norm(0)
            dense = 0
            norms = 1
            for k, (src, layers, fn) in enumerate(PROPS):
                if src == "x":
                    pe.wait_ge(x_ready, NC * norms)
                elif fn == "leaky":
                    pe.wait_ge(leaky_done, lk_before(dense))
                else:
                    pe.wait_ge(act_done, dense)
                naturals(k, xT if src == "x" else out_sb)
                for st, c in wave(len(layers)):
                    cs = slice(C0[c], C0[c] + CW[c])
                    if st == 0:
                        if k and c == 0:
                            pe.wait_ge(agg_read, NC * k)
                        for t in range(T):
                            if c == 0 and t in (0, 4, 8):
                                pe.wait_ge(nat_read, NC * k + t // 4 + 1)
                            last = nc.tensor.matmul(ps[:, c, 0:CW[c]], nat[0:KROWS, t, :], adjT[0:KROWS, t, cs],
                                                    start=(t == 0), stop=(t == T - 1))
                        last.then_inc(agg_ready, 1)
                        continue
                    if st == 1:
                        pe.wait_ge(agg_read, NC * k + c + 1)
                        rhs = z_sb
                    else:
                        pe.wait_ge(leaky_done, lk_before(dense_index(k, st - 1, c)) + 1)
                        rhs = mid[st - 2]
                    if dense >= 2:
                        pe.wait_ge(act_done, dense - 1)
                    nc.tensor.matmul(ps[:, 3 + dense % 2, 0:CW[c]], wts[:, layers[st - 1], :], rhs[:, cs], start=True,
                                     stop=True).then_inc(dense_ready, 1)
                    dense += 1
                if k in NORM_AFTER:
                    norm(NORM_AFTER[k])
                    norms += 1
            pe.wait_ge(x_ready, NC * norms)
            naturals(len(PROPS), xT)


def dense_index(k, st, c):
    before = sum(NC * len(layers) for _, layers, _ in PROPS[:k])
    order = [x for x in wave(len(PROPS[k][1])) if x[0]]
    return before + order.index((st, c))


def lk_before(dense):
    n = 0
    total = 0
    for _, layers, fn in PROPS:
        size = NC * len(layers)
        take = min(size, max(0, dense - total))
        if fn == "leaky":
            n += take
        total += size
    return n


_WEIGHTS = ["L1_gnn_W", "L2_gnn_kernel"] + [f"L3_gnn_{d}_W{i}" for d in ("uv", "vu") for i in (1, 2, 3)]
_BIASES = ["L1_gnn_b", "L2_gnn_bias"] + [f"L3_gnn_{d}_b{i}" for d in ("uv", "vu") for i in (1, 2, 3)]


def kernel(**inputs):
    import numpy as np
    import concourse.bacc as bacc
    from concourse.bass_utils import run_bass_kernel_spmd

    nc = bacc.Bacc("TRN2", target_bir_lowering=False, num_devices=1)
    arrays = {}

    def arg(name):
        a = np.ascontiguousarray(inputs[name])
        arrays["in_" + name] = a
        return nc.dram_tensor("in_" + name, a.shape, mybir.dt.from_np(a.dtype), kind="ExternalInput").ap()

    x, adj = arg("x"), arg("adj")
    wqkv = [arg("L0_gnn_W" + n) for n in "qkv"]
    wo = arg("L0_gnn_Wo")
    weights = [arg(n) for n in _WEIGHTS]
    biases = [arg(n) for n in _BIASES]
    out = nc.dram_tensor("out", (N, D), F32, kind="ExternalOutput").ap()
    build(nc, x, adj, wqkv, wo, weights, biases, out)
    r = run_bass_kernel_spmd(nc, [arrays], core_ids=[0])
    return r.results[0]["out"]
```

```python
from contextlib import ExitStack

import concourse.bass as bass
from concourse import mybir

F32 = mybir.dt.float32
BF16 = mybir.dt.bfloat16
ALU = mybir.AluOpType
ACT = mybir.ActivationFunctionType
AX = mybir.AxisListType

N = 1354
D = 128
H = 8
P = 128
T = -(-N // P)
NPAD = T * P
KROWS = -(-N // T)
NKEYS = [KROWS if t < N - T * (KROWS - 1) else KROWS - 1 for t in range(T)]
RP = [min(P, N - P * i) for i in range(T)]
G = N * D
SCALE = float(D) ** -0.5
EPS = 1e-5

HG = 4
NG = D // HG
CW = [452, 452, 450]
C0 = [0, 452, 904]
MW = 452
M0 = [0, 451, 902]
NC = len(CW)
STEPS = NC * T
PAIRS = HG * T * NC // 2
BATCHES = [(0, 4), (4, 4), (8, T - 8)]
SLOTS = PAIRS + len(BATCHES)
PARTS = 3
SPLITS = 3
SROWS = PARTS * PARTS * H
ZROWS = 96
MAXROWS = ZROWS + PARTS
ALLROWS = MAXROWS + PARTS
V1 = H + 1

RING = 6
LAG = 5
ACT_LEAD = RING
DVE_LEAD = RING
EARLY = (3, 10)
AHEAD = 17
ADD, MUL = "a", "m"
KIND = "mammamammmamammmmmammmmammammaamm"
assert len(KIND) == STEPS
ADDS, MULS = KIND.count(ADD), KIND.count(MUL)
PAIRS_IN = [0 if kind == ADD else (m + 1) * PAIRS // MULS - m * PAIRS // MULS
            for kind, m in zip(KIND, [KIND[:s].count(MUL) for s in range(STEPS)])]
PASS_PAIRS = [PAIRS_IN[(w - AHEAD) % STEPS] for w in range(STEPS)]
PAIR_FROM = [sum(PASS_PAIRS[:w]) for w in range(STEPS + 1)]
BATCH_END = [next(w for w in range(STEPS) if 2 * PAIR_FROM[w] >= (i + n) * HG * NC) for i, n in BATCHES[:-1]] + [STEPS]
PLANS = {ADD: {0: "012V3"}, MUL: {2: "P01P23V", 3: "P0P12P3V", 4: "P0P1P2P3V"}}


def early_steps(i):
    first, steps = EARLY
    if i < first:
        return range(0)
    return range((i - first) * steps // (T - first), (i + 1 - first) * steps // (T - first))


def slot_of(z):
    g, w = divmod(z, STEPS)
    return 0 if z == 0 else SLOTS * g + PAIR_FROM[w] + sum(w > e for e in [0] + BATCH_END[:-1]) - 1


def batch_before(z):
    g, w = divmod(z, STEPS)
    if z and w == 0:
        return len(BATCHES) * g - 1
    return len(BATCHES) * g + BATCH_END.index(w) if w in BATCH_END else None


def plan(u, maxing):
    p = 9
    items = []
    for x in PLANS[kind(u)][PAIRS_IN[u % STEPS]]:
        if x != "P":
            items.append(x)
        elif maxing:
            p += 1
            items.append(p)
    return items


def adds_before(u):
    return u // STEPS * ADDS + KIND[: u % STEPS].count(ADD)


def muls_before(u):
    return u // STEPS * MULS + KIND[: u % STEPS].count(MUL)


def slot(u):
    return u % (2 * STEPS) % RING


def last_user(u):
    return next(v for v in range(u - 1, u - 2 * RING - 1, -1) if slot(v) == slot(u))


def kind(u):
    return KIND[u % STEPS]


UV, VU = (2, 3, 4), (5, 6, 7)
PROPS = [("x", (0,), "silu"), ("out", (0,), "silu"), ("x", (1,), "relu"),
         ("x", UV, "leaky"), ("out", VU, "leaky"), ("out", UV, "leaky"), ("out", VU, "leaky"), ("out", UV, "leaky")]
NORM_AFTER = {1: 1, 2: 2, 7: 3}
NORMS = 1 + len(NORM_AFTER)
FROM_NORM = [k for k, prop in enumerate(PROPS) if prop[0] == "x"] + [len(PROPS)]


def wave(layers):
    return [(st, c - st) for c in range(NC + layers) for st in range(layers + 1) if 0 <= c - st < NC]


def build(nc, x, adj, wqkv, wo, weights, biases, out):
    ctx = ExitStack()
    with ctx:
        def sem(name):
            return ctx.enter_context(nc.semaphore(name))

        def sb(name, shape, dt):
            return ctx.enter_context(nc.sbuf_tensor(name, shape, dt))

        qk_parts = nc.dram_tensor("qk_parts", [2, PARTS, H, G], BF16, kind="Internal").ap()
        v_rows = nc.dram_tensor("v_rows", [G * V1], F32, kind="Internal").ap()
        x_cols = nc.dram_tensor("x_cols", [D, N], F32, kind="Internal").ap()
        max_rows = [nc.dram_tensor(f"max_rows{b}", [PARTS, HG * n, P], BF16, kind="Internal").ap()
                    for b, (_, n) in enumerate(BATCHES)]
        att = nc.dram_tensor("att", [V1, G], F32, kind="Internal").ap()

        adjT = sb("adjT", [P, T, N], F32)
        ident = sb("ident", [P, P], F32)
        v_sb = sb("v_sb", [P, 2, HG, T * V1], F32)
        o_sb = sb("o_sb", [P, 2, 452], F32)
        maxes = sb("maxes", [P, 2 * PAIRS], F32)
        negmax = sb("negmax", [P, P], F32)
        rowrem = sb("rowrem", [16, P], F32)
        rowparts = sb("rowparts", [16, len(BATCHES), PARTS, P], BF16)
        biasrow = sb("biasrow", [PARTS, NPAD], BF16)
        ones3 = sb("ones3", [PARTS, KROWS], BF16)
        epst = sb("epst", [P, 1], F32)
        avg = sb("avg", [P, P], F32)

        EBSZ = MULS * 452
        QSZ, KSZ = 2 * HG * NPAD // 2, 2 * HG * N // 2
        RSZ = RING * HG * 452
        arena = sb("arena", [P, EBSZ + QSZ + KSZ + RSZ], F32)
        EB0, Q0, K0, R0 = 0, EBSZ, EBSZ + QSZ, EBSZ + QSZ + KSZ

        def carve(at, shape, rows=P, dt=F32):
            size = 1
            for n in shape:
                size *= n
            words = size if dt == F32 else size // 2
            v = arena[0:rows, at:at + words]
            if dt != F32:
                v = v.bitcast(dt)
            if len(shape) == 1:
                return v
            names = "abcd"[: len(shape)]
            return v.rearrange(f"p ({' '.join(names)}) -> p {' '.join(names)}",
                               **{k: n for k, n in zip(names, shape)})

        ebias = carve(EB0, [MULS, 452])
        q_sb = carve(Q0, [2, HG, NPAD], P, BF16)
        k_sb = carve(K0, [2, HG, N], P, BF16)
        ring = carve(R0, [RING, HG, 452])

        x_nat = carve(EB0, [T, D])
        wT = carve(EB0 + T * D, [3, 1024])
        rem = [carve(EB0 + T * D + 3072 + 1024 * i, [1024]) for i in range(SPLITS)]
        w_nat = carve(R0, [3, H, D])
        parts = [carve(R0 + 3072 + 1536 * i, [PARTS, 1024], P, BF16) for i in range(SPLITS)]
        VO0, VO1 = 3072 + 1536 * SPLITS, T * D + 3072 + 1024 * SPLITS
        v_out = [carve(R0 + VO0, [P, V1]), carve(EB0 + VO1, [P, V1])]
        xT0 = carve(R0 + VO0 + P * V1, [NPAD])
        adj_nat = [carve(R0 + NPAD * i, [NPAD]) for i in range(2)]
        assert VO0 + P * V1 + NPAD <= RSZ and VO1 + P * V1 <= EBSZ and 2 * NPAD <= 3072

        at = 0
        oT = carve(0, [H, N]); at += H * N
        o_nat = [carve(at + V1 * P * i, [V1, P]) for i in range(3)]; at += 3 * V1 * P
        rsum = [carve(at + P * i, [P]) for i in range(2)]; at += 2 * P
        z_sb = carve(at, [N]); at += N
        mid = [carve(at + N * i, [N]) for i in range(2)]; at += 2 * N
        leak = carve(at, [N]); at += N
        out_sb = carve(at, [NPAD]); at += NPAD
        cen = carve(at, [NPAD]); at += NPAD
        sq = carve(at, [NPAD]); at += NPAD
        dev = carve(0, [N])
        rstd = carve(at, [T]); at += T
        nat = carve(at, [T, D]); at += T * D
        xT = carve(at, [NPAD]); at += NPAD
        wo_nat = carve(at, [D * H]); at += D * H
        woT = carve(at, [H, D]); at += H * D
        wts = carve(at, [8, D]); at += 8 * D
        bia = carve(at, [8]); at += 8
        assert at <= EBSZ + QSZ + KSZ + RSZ

        ps = ctx.enter_context(nc.psum_tensor("ps", [P, 8, 512], F32))
        ST_BANK, PV_BANK = 4, 7

        s_ident = sem("s_ident")
        w_loaded = [sem(f"w_loaded{i}") for i in range(3)]
        x_loaded = sem("x_loaded")
        small_loaded = sem("small_loaded")
        fill = sem("fill")
        spare_rows = sem("spare_rows")
        wt_ready = sem("wt_ready")
        wt_read = sem("wt_read")
        proj_ready = sem("proj_ready")
        proj_read = sem("proj_read")
        rem1_ready = sem("rem1_ready")
        part2_ready = sem("part2_ready")
        part3_ready = sem("part3_ready")
        parts_stored = [sem(f"parts_stored{i}") for i in range(SPLITS)]
        v_stored = [sem(f"v_stored{i}") for i in range(2)]
        adj_loaded = [sem(f"adj_loaded{i}") for i in range(2)]
        adjt_ready = sem("adjt_ready")
        adjt_read = sem("adjt_read")
        bmax_ready = sem("bmax_ready")
        brow_ready = sem("brow_ready")
        brow_step = sem("brow_step")
        brow_copied = sem("brow_copied")
        brow_spread = sem("brow_spread")
        bb_ready = sem("bb_ready")
        eb_sum = sem("eb_sum")
        eb_ready = sem("eb_ready")
        negmax_clear = sem("negmax_clear")
        qk_loaded = [sem(f"qk_loaded{i}") for i in range(2)]
        v_loaded = [sem(f"v_loaded{i}") for i in range(2)]
        maxrow_loaded = [sem(f"maxrow_loaded{i}") for i in range(len(BATCHES))]
        maxrow_stored = sem("maxrow_stored")
        s_ready = sem("s_ready")
        s_read = sem("s_read")
        negmax_ready = sem("negmax_ready")
        split_step = sem("split_step")
        st_ready = sem("st_ready")
        exps_done = sem("exps_done")
        adds_done = sem("adds_done")
        sbexp_done = sem("sbexp_done")
        mults_done = sem("mults_done")
        pv_done = sem("pv_done")
        o_copied = sem("o_copied")
        o_stored = [sem(f"o_stored{i}") for i in range(2)]
        xt_stored = sem("xt_stored")
        xt_loaded = sem("xt_loaded")
        wo_loaded = sem("wo_loaded")
        wot_ready = sem("wot_ready")
        wot_read = sem("wot_read")
        on_loaded = [sem(f"on_loaded{i}") for i in range(3)]
        rsum_ready = sem("rsum_ready")
        on_ready = sem("on_ready")
        ot_ready = sem("ot_ready")
        ot_read = sem("ot_read")
        y_ready = sem("y_ready")
        z_ready = sem("z_ready")
        mean_ready = sem("mean_ready")
        cen_ready = sem("cen_ready")
        sq_ready = sem("sq_ready")
        var_ready = sem("var_ready")
        std_ready = sem("std_ready")
        inv_ready = sem("inv_ready")
        x_ready = sem("x_ready")
        nodevar_ready = sem("nodevar_ready")
        nodestd_ready = sem("nodestd_ready")
        nodeinv_ready = sem("nodeinv_ready")
        nat_ready = sem("nat_ready")
        nat_read = sem("nat_read")
        agg_ready = sem("agg_ready")
        agg_read = sem("agg_read")
        dense_ready = sem("dense_ready")
        act_done = sem("act_done")
        leaky_done = sem("leaky_done")
        out_stored = sem("out_stored")

        block = ctx.enter_context(nc.Block())

        PROJ_BANK, ADJ_BANK = 4, 6
        VAR_BANK = [3, 4, 1]
        N_ADJ = 3
        TB = [(0, 4), (4, 4), (8, T - 8)]

        @block.sync
        def _(sp):
            sp.dma_start(w_nat[:, 0, :, :], wqkv[0].rearrange("(j h) c -> j h c", h=H)).then_inc(w_loaded[0], 16)
            sp.dma_start(x_nat[:, 0:T - 1, :], x[0:(T - 1) * P, :].rearrange("(i p) d -> p i d", p=P)).then_inc(x_loaded, 16)
            sp.dma_start(x_nat[0:RP[-1], T - 1, :], x[(T - 1) * P:N, :]).then_inc(x_loaded, 16)
            for w in (1, 2):
                sp.dma_start(w_nat[:, w, :, :], wqkv[w].rearrange("(j h) c -> j h c", h=H)).then_inc(w_loaded[w], 16)
            def load_adj(i):
                if i == 0:
                    sp.wait_ge(wt_ready, 9)
                    sp.wait_ge(wt_read, 9)
                    sp.dma_start(x_cols, xT0[:, 0:N]).then_inc(xt_stored, 16)
                if i >= 2:
                    sp.wait_ge(adjt_ready, N_ADJ * (i - 1))
                    sp.wait_ge(bmax_ready, i - 1)
                sp.dma_start(adj_nat[i % 2][0:RP[i], 0:N], adj[P * i:P * i + RP[i], :]).then_inc(adj_loaded[i % 2], 16)

            def load_qk(g, par):
                for b in range(PARTS):
                    sp.dma_start(q_sb[24 * b:24 * b + 24, par, :, 0:N],
                                 qk_parts[0].rearrange("k h g -> (k h) g")[:, bass.ds(g * (HG * N), HG * N)]
                                 .rearrange("r (a n) -> r a n", a=HG)).then_inc(qk_loaded[par], 16)
                    for a in range(PARTS):
                        sp.dma_start(k_sb[24 * b + 8 * a:24 * b + 8 * a + 8, par, :, :].rearrange("r a n -> r (a n)"),
                                     qk_parts[1, b, :, bass.ds(g * (HG * N), HG * N)]).then_inc(qk_loaded[par], 16)

            def load_v(g, par):
                src = v_rows[bass.ds(g * (HG * N * V1), HG * N * V1)].rearrange("(a m) -> a m", a=HG)
                full = (KROWS - 1) * T * V1
                sp.dma_start(v_sb[0:KROWS - 1, par, :, :],
                             src[:, 0:full].rearrange("a (p x) -> p a x", x=T * V1)).then_inc(v_loaded[par], 16)
                sp.dma_start(v_sb[KROWS - 1:KROWS, par, :, 0:V1], src[:, full:full + V1].rearrange("(o a) x -> o a x", o=1)).then_inc(v_loaded[par], 16)

            for i in range(2):
                load_adj(i)
            assert 2 * HG * N <= P * P and SPLITS >= 2
            for i in range(T):
                r = RP[i]
                for w in range(2):
                    e = 2 * i + w
                    sp.wait_ge(part3_ready, e + 1)
                    for k in range(PARTS):
                        sp.dma_start(qk_parts[w, k, :, P * P * i:P * P * i + r * P].rearrange("h (r j) -> r h j", j=P),
                                     parts[e % SPLITS][0:r, k, :].rearrange("p (h j) -> p h j", h=H)).then_inc(parts_stored[e % SPLITS], 16)
                    if w == 0 and 2 <= i + 1 < T:
                        load_adj(i + 1)
                sp.wait_ge(proj_read, 6 * i + 6)
                sp.dma_start(v_rows[P * P * V1 * i:P * V1 * (P * i + r)].rearrange("(r j) -> r j", j=P * V1),
                             v_out[i % 2][0:r, :, :].rearrange("p j h -> p (j h)")).then_inc(v_stored[i % 2], 16)
                if i in (1, 5):
                    for n in range(2):
                        sp.wait_ge(parts_stored[n], 48)
                    sp.wait_ge(v_stored[0], 16)
                    sp.wait_ge(spare_rows, 5)
                    load_qk(i // 5, i // 5)
                    load_v(i // 5, i // 5)
            for i in range(SPLITS):
                sp.wait_ge(parts_stored[i], 48 * len(range(i, 2 * T, SPLITS)))
            for i in range(2):
                sp.wait_ge(v_stored[i], 16 * len(range(i, T, 2)))

            def maxrows(it, beta):
                gbase, b = divmod(beta, len(BATCHES))
                i0, n = BATCHES[b]
                sp.wait_ge(split_step, it * (6 * len(BATCHES)) + (3 * beta + 3))
                sp.dma_start(max_rows[b].rearrange("k x j -> x k j"), rowparts[0:HG * n, b, :, :]).then_inc(maxrow_stored, 16)
                sp.wait_ge(maxrow_stored, it * (32 * len(BATCHES)) + 16 * (beta + 1))
                sp.dma_start(q_sb[ZROWS:MAXROWS, gbase % 2, :, P * i0:P * (i0 + n)],
                             max_rows[b].rearrange("k (a i) j -> k a (i j)", a=HG)).then_inc(maxrow_loaded[b], 16)

            def store(g, q, c, cnt):
                sp.wait_ge(o_copied, cnt + 1)
                for a in range(HG):
                    sp.dma_start(att[:, bass.ds(g * (HG * N) + (a * N + C0[c]), CW[c])],
                                 o_sb[32 * a:32 * a + V1, q % 2, 0:CW[c]]).then_inc(o_stored[q % 2], 16)

            sp.wait_ge(brow_step, 4)
            for k in range(PARTS):
                sp.dma_start(biasrow[k:k + 1, :].rearrange("o (i j) -> o i j", j=P), rowparts[0:T, 0, k, :]).then_inc(brow_copied, 16)
            sp.wait_ge(brow_copied, 16 * PARTS)
            sp.dma_start(q_sb[MAXROWS:ALLROWS, :, :, :].rearrange("k g a n -> k (g a) n"),
                         biasrow[:].unsqueeze(1).to_broadcast([PARTS, 2 * HG, NPAD])).then_inc(brow_spread, 16)
            sp.wait_ge(brow_spread, 16)
            maxrows(0, 0)

            def group(it, par, more_qk, more_max):
                g = it * 2 + par
                for c in range(NC - 1):
                    maxrows(it, 3 * par + c + 1)
                    store(g, NC * par + c, c, it * (2 * NC) + (NC * par + c + 1))
                if more_max:
                    maxrows(it, 3 * par + 3)
                if more_qk:
                    sp.wait_ge(st_ready, it * (2 * HG * STEPS) + HG * STEPS * (par + 1))
                    load_qk(g + 2, par)
                store(g, NC * par + 2, 2, it * (2 * NC) + (NC * par + 3))
                if more_qk:
                    sp.wait_ge(pv_done, it * (2 * STEPS) + STEPS * (par + 1))
                    load_v(g + 2, par)

            with sp.Fori(0, NG // 2 - 1) as it:
                group(it, 0, True, True)
                group(it, 1, True, True)
            group(NG // 2 - 1, 0, False, True)
            group(NG // 2 - 1, 1, False, False)
            for i in range(2):
                sp.wait_ge(o_stored[i], 64 * (NG // 2) * NC + 16)
            sp.wait_ge(xt_stored, 16)
            for i in range(T):
                if i == 3:
                    sp.dma_start(wo_nat, wo).then_inc(wo_loaded, 16)
                if i >= 3:
                    sp.wait_ge(ot_ready, 2 * (i - 2))
                sp.dma_start(o_nat[i % 3][0:RP[i], :, :],
                             att[:, P * P * i:P * P * i + P * RP[i]].rearrange("h (r j) -> r h j", j=P)).then_inc(on_loaded[i % 3], 16)
            sp.dma_start(xT[:, 0:N], x_cols).then_inc(xt_loaded, 16)
            for n in range(8):
                sp.dma_start(wts[:, n, :], weights[n]).then_inc(small_loaded, 16)
                sp.dma_start(bia[:, n:n + 1], biases[n].rearrange("(d o) -> d o", o=1)).then_inc(small_loaded, 16)
            sp.wait_ge(nat_read, NC * (len(PROPS) + 1))
            full = (KROWS - 1) * T
            sp.dma_start(out[0:full, :].rearrange("(p t) d -> p t d", t=T), nat[0:KROWS - 1, :, :]).then_inc(out_stored, 16)
            sp.dma_start(out[full:N, :], nat[KROWS - 1:KROWS, 0, :]).then_inc(out_stored, 16)
            sp.wait_ge(out_stored, 32)

        @block.gpsimd
        def _(pool):
            nc.gpsimd.memset(ident[:], 0.0).then_inc(s_ident, 1)
            pool.wait_ge(s_ident, 1)
            nc.gpsimd.affine_select(out=ident[:], in_=ident[:], compare_op=ALU.not_equal, fill=1.0, base=0,
                                    pattern=[[-1, P]], channel_multiplier=1).then_inc(s_ident, 1)
            fills = [(q_sb[0:64, :, :, N:NPAD], 0.0), (q_sb[64:96, :, :, :], 0.0), (k_sb[64:96, :, :, :], 0.0),
                     (k_sb[96:128, :, :, :], 1.0), (v_sb[:], 0.0)]
            for n, (dst, value) in enumerate(fills):
                if n:
                    pool.wait_ge(spare_rows, n)
                nc.gpsimd.memset(dst, value).then_inc(spare_rows, 1)
            pool.wait_ge(eb_ready, MULS)

            def mults(it, u):
                c, t = divmod(u % STEPS, T)
                pool.wait_ge(exps_done, it * (2 * HG * MULS) + HG * (muls_before(u) + 1))
                w = ring[0:NKEYS[t], slot(u), :, 0:CW[c]]
                e = ebias[0:NKEYS[t], muls_before(u % STEPS), 0:CW[c]].unsqueeze(1).to_broadcast([NKEYS[t], HG, CW[c]])
                nc.gpsimd.tensor_tensor(w, w, e, ALU.mult).then_inc(mults_done, 1)

            with pool.Fori(0, NG // 2) as it:
                for u in range(2 * STEPS):
                    if kind(u) == MUL:
                        mults(it, u)

        @block.scalar
        def _(act):
            for b in range(9):
                act.wait_ge(wt_ready, b + 1)
                if b < 3:
                    a = 512 * b
                    w = min(512, N - a)
                    nc.scalar.activation(xT0[:, a:a + w], ps[:, b % 8, 0:w], ACT.Copy).then_inc(wt_read, 1)
                else:
                    dst = wT[:, (b - 3) // 2, 512 * ((b - 3) % 2):512 * ((b - 3) % 2) + 512]
                    nc.scalar.activation(dst, ps[:, b % 8, :], ACT.Copy).then_inc(wt_read, 1)
            def second(e):
                r = RP[e // 2]
                act.wait_ge(rem1_ready, e + 1)
                nc.scalar.activation(parts[e % SPLITS][0:r, 1, :], rem[e % SPLITS][0:r, :], ACT.Copy).then_inc(part2_ready, 1)

            for i in range(T):
                r = RP[i]
                for w in range(3):
                    s = 3 * i + w
                    if w < 2:
                        e = 2 * i + w
                        sc = SCALE if w == 0 else 1.0
                        if e >= SPLITS:
                            act.wait_ge(part3_ready, e - SPLITS + 1)
                            act.wait_ge(parts_stored[e % SPLITS], 48 * (e // SPLITS))
                    elif i == 0:
                        act.wait_ge(fill, 1)
                    elif i >= 2:
                        act.wait_ge(v_stored[i % 2], 16 * (i // 2))
                    for h in range(2):
                        src = ps[0:r, PROJ_BANK + h, :]
                        act.wait_ge(proj_ready, 2 * s + h + 1)
                        if w < 2:
                            cols = slice(512 * h, 512 * h + 512)
                            nc.scalar.activation(rem[e % SPLITS][0:r, cols], src, ACT.Copy, scale=sc)
                            nc.scalar.activation(parts[e % SPLITS][0:r, 0, cols], src, ACT.Copy, scale=sc).then_inc(proj_read, 1)
                        else:
                            nc.scalar.activation(v_out[i % 2][0:r, :, 4 * h:4 * h + 4].rearrange("p j h -> p h j"),
                                                 src.rearrange("p (h j) -> p h j", h=4), ACT.Copy).then_inc(proj_read, 1)
                    if w:
                        second(2 * i + w - 1)
                for b, (t0, nt) in enumerate(TB):
                    n = N_ADJ * i + b
                    act.wait_ge(adjt_ready, n + 1)
                    nc.scalar.activation(adjT[0:KROWS, t0:t0 + nt, P * i:P * i + RP[i]],
                                         ps[0:KROWS, ADJ_BANK + n % 2, :].rearrange("p (t n) -> p t n", n=P)[:, 0:nt, 0:RP[i]],
                                         ACT.Copy).then_inc(adjt_read, 1)
            for m in range(MULS):
                act.wait_ge(eb_sum, m + 1)
                s = [s for s in range(STEPS) if kind(s) == MUL][m]
                e = ebias[0:NKEYS[s % T], m, 0:CW[s // T]]
                nc.scalar.activation(e, e, ACT.Exp).then_inc(eb_ready, 1)

            def exps(it, u):
                c, t = divmod(u % STEPS, T)

                if kind(u) == ADD:
                    return
                if last_user(u) >= 0 or not isinstance(it, int) or it > 0:
                    act.wait_ge(pv_done, it * (2 * STEPS) + (last_user(u) + 1))
                for a in range(HG):
                    j = HG * u + a
                    act.wait_ge(st_ready, it * (2 * HG * STEPS) + (j + 1))
                    nc.scalar.activation(ring[0:NKEYS[t], slot(u), a, 0:CW[c]], ps[0:NKEYS[t], ST_BANK + j % 3, 0:CW[c]],
                                         ACT.Exp).then_inc(exps_done, 1)

            def sbexps(it, u):
                if kind(u) != ADD:
                    return
                c, t = divmod(u % STEPS, T)
                act.wait_ge(adds_done, it * (2 * HG * ADDS) + HG * (adds_before(u) + 1))
                w = ring[0:NKEYS[t], slot(u), :, 0:CW[c]]
                nc.scalar.activation(w, w, ACT.Exp).then_inc(sbexp_done, 1)

            def copy_sums(it, q):
                act.wait_ge(pv_done, it * (2 * STEPS) + T * (q + 1))
                act.wait_ge(o_stored[q % 2], it * (64 * NC) + (64 * (q // 2) + 16))
                nc.scalar.activation(o_sb[0:96 + V1, q % 2, 0:CW[q % NC]], ps[0:96 + V1, PV_BANK, 0:CW[q % NC]],
                                     ACT.Copy).then_inc(o_copied, 1)

            for u in range(ACT_LEAD):
                exps(0, u)
                if u:
                    sbexps(0, u - 1)

            def body(it, last):
                for xx in range(2 * STEPS):
                    u = xx + ACT_LEAD
                    if xx % T == T - 1:
                        copy_sums(it, xx // T)
                    if u < 2 * STEPS or not last:
                        exps(it, u)
                    if u - 1 < 2 * STEPS or not last:
                        sbexps(it, u - 1)

            with act.Fori(0, NG // 2 - 1) as it:
                body(it, False)
            body(NG // 2 - 1, True)

            for i in range(T):
                for b in range(2 if i == 3 else 0):
                    act.wait_ge(wot_ready, b + 1)
                    nc.scalar.activation(woT[:, 4 * b:4 * b + 4, :].rearrange("p h d -> p (h d)"), ps[:, 6 + b, :],
                                         ACT.Copy).then_inc(wot_read, 1)
                for b in range(2):
                    n = 2 * i + b
                    act.wait_ge(ot_ready, n + 1)
                    nc.scalar.activation(oT[:, 4 * b:4 * b + 4, P * i:P * i + RP[i]],
                                         ps[:, n % 6, :].rearrange("p (h n) -> p h n", n=P)[:, :, 0:RP[i]],
                                         ACT.Copy).then_inc(ot_read, 1)

            def norm(k):
                for c in range(NC):
                    act.wait_ge(cen_ready, NC * k + c + 1)
                    cs = slice(C0[c], C0[c] + CW[c])
                    nc.scalar.activation(sq[:, cs], cen[:, cs], ACT.Square).then_inc(sq_ready, 1)
                act.wait_ge(nodevar_ready, k + 1)
                nc.scalar.activation(rstd[0:KROWS, :], ps[0:KROWS, 2, 0:T], ACT.Sqrt, bias=epst[0:KROWS, :]).then_inc(nodestd_ready, 1)
                for c in range(NC if k < NORMS - 1 else 0):
                    act.wait_ge(var_ready, NC * k + c + 1)
                    nc.scalar.activation(dev[:, C0[c]:C0[c] + CW[c]], ps[:, VAR_BANK[c], 0:CW[c]], ACT.Sqrt,
                                         bias=epst[:]).then_inc(std_ready, 1)

            def naturals(k):
                for b, (t0, nt) in enumerate(TB):
                    n = NC * k + b
                    act.wait_ge(nat_ready, n + 1)
                    nc.scalar.activation(nat[0:KROWS, t0:t0 + nt, :],
                                         ps[0:KROWS, 5 + b, 0:nt * D].rearrange("p (t d) -> p t d", d=D),
                                         ACT.Copy).then_inc(nat_read, 1)

            norm(0)
            dense = 0
            for k, (src, layers, fn) in enumerate(PROPS):
                if k not in FROM_NORM:
                    naturals(k)
                for st, c in wave(len(layers)):
                    cs = slice(C0[c], C0[c] + CW[c])
                    if st == 0:
                        act.wait_ge(agg_ready, NC * k + c + 1)
                        nc.scalar.activation(z_sb[:, cs], ps[:, c, 0:CW[c]], ACT.Copy).then_inc(agg_read, 1)
                        continue
                    act.wait_ge(dense_ready, dense + 1)
                    src_ps = ps[:, 3 + dense % 2, 0:CW[c]]
                    b = bia[:, layers[st - 1]:layers[st - 1] + 1]
                    if fn == "leaky":
                        nc.scalar.activation(leak[:, cs], src_ps, ACT.Identity, bias=b).then_inc(act_done, 1)
                    else:
                        nc.scalar.activation(out_sb[:, cs], src_ps, ACT.Silu if fn == "silu" else ACT.Relu, bias=b).then_inc(act_done, 1)
                    dense += 1
                if k in NORM_AFTER:
                    norm(NORM_AFTER[k])

        @block.vector
        def _(dve):
            def max_pair(it, z, p):
                sl = slot_of(z) + p
                col = 2 * (PAIR_FROM[z % STEPS] + p)
                dve.wait_ge(s_ready, it * (2 * SLOTS) + (sl + 1))
                nc.vector.tensor_reduce(maxes[:, col:col + 2], ps[:, 2 * (sl % 2):2 * (sl % 2) + 2, 0:MW], op=ALU.max,
                                        axis=AX.X).then_inc(s_read, 1)

            def third(e):
                r = RP[e // 2]
                dve.wait_ge(part2_ready, e + 1)
                nc.vector.tensor_tensor(parts[e % SPLITS][0:r, 2, :], rem[e % SPLITS][0:r, :], parts[e % SPLITS][0:r, 1, :],
                                        ALU.subtract).then_inc(part3_ready, 1)

            nc.vector.memset(v_out[0][:, :, H:V1], 1.0)
            nc.vector.memset(v_out[1][:, :, H:V1], 1.0)
            nc.vector.memset(avg[:], 1.0 / D)
            nc.vector.memset(epst[:], EPS)
            nc.vector.memset(ones3[:], 1.0).then_inc(fill, 1)
            for i in range(2):
                nc.vector.memset(o_sb[:, i, :], 0.0).then_inc(o_stored[i], 16)
            for b in range(len(BATCHES)):
                nc.vector.memset(rowparts[:, b, :, :], 0.0).then_inc(maxrow_loaded[b], 16)
            dve.wait_ge(wt_ready, 9)
            for i in range(2):
                nc.vector.memset(adj_nat[i][:, N:NPAD], 0.0).then_inc(fill, 1)
            nc.vector.memset(negmax[:], 0.0).then_inc(negmax_clear, 1)
            dve.wait_ge(negmax_clear, 1)
            for e in range(2 * T):
                i, w = divmod(e, 2)
                r = RP[i]
                dve.wait_ge(proj_read, 2 * (3 * i + w) + 2)
                nc.vector.tensor_tensor(rem[e % SPLITS][0:r, :], rem[e % SPLITS][0:r, :], parts[e % SPLITS][0:r, 0, :],
                                        ALU.subtract).then_inc(rem1_ready, 1)
                if w == 1:
                    third(e - 1)
                    third(e)
                    dve.wait_ge(adj_loaded[i % 2], 16 * (i // 2 + 1))
                    nc.vector.tensor_reduce(negmax[0:RP[i], i:i + 1], adj_nat[i % 2][0:RP[i], 0:N], op=ALU.max,
                                            axis=AX.X, negate=True).then_inc(bmax_ready, 1)
                    for z in early_steps(i):
                        for p in range(PASS_PAIRS[z]):
                            max_pair(0, z, p)
            dve.wait_ge(brow_ready, 1)
            nc.vector.tensor_scalar(rowparts[0:T, 0, 0, :], ps[0:T, 7, 0:P], 2.0, None, ALU.mult).then_inc(brow_step, 1)
            dve.wait_ge(brow_step, 1)
            nc.vector.scalar_tensor_tensor(out=rowrem[0:T, :], in0=ps[0:T, 7, 0:P], scalar=2.0, in1=rowparts[0:T, 0, 0, :],
                                           op0=ALU.mult, op1=ALU.subtract).then_inc(brow_step, 1)
            dve.wait_ge(brow_step, 2)
            nc.vector.tensor_copy(rowparts[0:T, 0, 1, :], rowrem[0:T, :]).then_inc(brow_step, 1)
            dve.wait_ge(brow_step, 3)
            nc.vector.tensor_tensor(rowparts[0:T, 0, 2, :], rowrem[0:T, :], rowparts[0:T, 0, 1, :], ALU.subtract).then_inc(brow_step, 1)
            def batch_max(it, z):
                beta = batch_before(z + 1)
                if beta is None:
                    return
                i0, n = BATCHES[beta % 3]
                dve.wait_ge(s_read, it * (2 * SLOTS) + (slot_of(z) + PASS_PAIRS[z % STEPS]))
                nc.vector.tensor_reduce(negmax[:, 0:HG * n].rearrange("p (a i) -> p i a", i=n),
                                        maxes[:, HG * NC * i0:HG * NC * (i0 + n)].rearrange("p (i a c) -> p i a c", a=HG, c=NC),
                                        op=ALU.max, axis=AX.X, negate=True).then_inc(negmax_ready, 1)

            def split_max(it, z, sl):
                beta = batch_before(z)
                gbase, b = divmod(beta, len(BATCHES))
                n = HG * BATCHES[b][1]
                src = ps[0:n, 2 * (sl % 2), 0:P]
                dve.wait_ge(s_ready, it * (2 * SLOTS) + (sl + 1))
                if isinstance(it, int) and it == 0 and beta == 0:
                    dve.wait_ge(brow_copied, 16 * PARTS)
                dve.wait_ge(maxrow_loaded[b], it * 32 + (16 * gbase + 16))
                nc.vector.tensor_copy(rowparts[0:n, b, 0, :], src).then_inc(split_step, 1)
                dve.wait_ge(split_step, it * (6 * len(BATCHES)) + (3 * beta + 1))
                nc.vector.tensor_tensor(rowrem[0:n, :], src, rowparts[0:n, b, 0, :], ALU.subtract).then_inc(s_read, 1)
                dve.wait_ge(s_read, it * (2 * SLOTS) + (sl + 1))
                nc.vector.tensor_copy(rowparts[0:n, b, 1, :], rowrem[0:n, :]).then_inc(split_step, 1)
                dve.wait_ge(split_step, it * (6 * len(BATCHES)) + (3 * beta + 2))
                nc.vector.tensor_tensor(rowparts[0:n, b, 2, :], rowrem[0:n, :], rowparts[0:n, b, 1, :],
                                        ALU.subtract).then_inc(split_step, 1)

            def add_bias(it, u, a):
                c, t = divmod(u % STEPS, T)
                if a == 0 and (last_user(u) >= 0 or not isinstance(it, int) or it > 0):
                    dve.wait_ge(pv_done, it * (2 * STEPS) + (last_user(u) + 1))
                j = HG * u + a
                dve.wait_ge(st_ready, it * (2 * HG * STEPS) + (j + 1))
                nc.vector.scalar_tensor_tensor(
                    out=ring[0:NKEYS[t], slot(u), a, 0:CW[c]], in0=adjT[0:NKEYS[t], t, C0[c]:C0[c] + CW[c]],
                    scalar=2.0, in1=ps[0:NKEYS[t], ST_BANK + j % 3, 0:CW[c]], op0=ALU.mult,
                    op1=ALU.add).then_inc(adds_done, 1)

            def step(it, u, maxing, scoring=True):
                z = u + AHEAD
                for x in plan(u, maxing) if scoring else [p + 10 for p in range(PASS_PAIRS[z % STEPS])]:
                    if not isinstance(x, str):
                        max_pair(it, z, x - 10)
                    elif x != "V" and kind(u) == ADD:
                        add_bias(it, u, int(x))
                if maxing:
                    batch_max(it, z)
                if batch_before(z) is not None and (maxing or z == 2 * STEPS):
                    split_max(it, z, slot_of(z) + (PASS_PAIRS[z % STEPS] if maxing else 0))

            for u in range(EARLY[1] - AHEAD, 0):
                step(0, u, True, False)
            dve.wait_ge(v_stored[1], 16 * len(range(1, T, 2)))
            dve.wait_ge(adjt_read, N_ADJ * T)
            for m, s in enumerate(s for s in range(STEPS) if kind(s) == MUL):
                c, t = divmod(s, T)
                dve.wait_ge(bb_ready, c + 1)
                nc.vector.scalar_tensor_tensor(out=ebias[0:NKEYS[t], m, 0:CW[c]], in0=adjT[0:NKEYS[t], t, C0[c]:C0[c] + CW[c]],
                                               scalar=2.0, in1=ps[0:NKEYS[t], ST_BANK + c, 0:CW[c]], op0=ALU.mult,
                                               op1=ALU.add).then_inc(eb_sum, 1)
            nc.vector.memset(ps[:, PV_BANK, :], 0.0).then_inc(o_copied, 1)

            for u in range(DVE_LEAD):
                step(0, u, True)
            with dve.Fori(0, NG // 2 - 1) as it:
                for xx in range(2 * STEPS):
                    step(it, xx + DVE_LEAD, True)
            for u in range(DVE_LEAD, 2 * STEPS):
                step(NG // 2 - 1, u, u + AHEAD < 2 * STEPS)

            for i in range(T):
                r = RP[i]
                dve.wait_ge(on_loaded[i % 3], 16 * (i // 3 + 1))
                o = o_nat[i % 3]
                if i >= 2:
                    dve.wait_ge(on_ready, i - 1)
                nc.vector.reciprocal(rsum[i % 2][0:r, :], o[0:r, H, :]).then_inc(rsum_ready, 1)
                dve.wait_ge(rsum_ready, i + 1)
                nc.vector.tensor_tensor(o[0:r, 0:H, :], o[0:r, 0:H, :], rsum[i % 2][0:r, :].unsqueeze(1).to_broadcast([r, H, P]),
                                        ALU.mult).then_inc(on_ready, 1)

            def norm(k, layer_chunk):
                def close(c):
                    cs = slice(C0[c], C0[c] + CW[c])
                    dve.wait_ge(std_ready, NC * k + c + 1)
                    nc.vector.reciprocal(dev[:, cs], dev[:, cs]).then_inc(inv_ready, 1)
                    dve.wait_ge(inv_ready, NC * k + c + 1)
                    nc.vector.tensor_tensor(xT[:, cs], cen[:, cs], dev[:, cs], ALU.mult).then_inc(x_ready, 1)

                for c in range(NC):
                    cs = slice(C0[c], C0[c] + CW[c])
                    y = layer_chunk(c)
                    if k:
                        dve.wait_ge(x_ready, NC * (k - 1) + c + 1)
                    nc.vector.tensor_tensor(z_sb[:, cs], y, xT[:, cs], ALU.add).then_inc(z_ready, 1)
                for c in range(NC):
                    cs = slice(C0[c], C0[c] + CW[c])
                    dve.wait_ge(mean_ready, NC * k + c + 1)
                    nc.vector.tensor_tensor(cen[:, cs], z_sb[:, cs], ps[:, 5 + c % 2, 0:CW[c]], ALU.subtract).then_inc(cen_ready, 1)
                dve.wait_ge(nodestd_ready, k + 1)
                nc.vector.reciprocal(rstd[0:KROWS, :], rstd[0:KROWS, :]).then_inc(nodeinv_ready, 1)
                dve.wait_ge(nodeinv_ready, k + 1)
                for b, (t0, nt) in enumerate(TB):
                    dve.wait_ge(nat_ready, NC * FROM_NORM[k] + b + 1)
                    nc.vector.tensor_tensor(nat[0:KROWS, t0:t0 + nt, :],
                                            ps[0:KROWS, 5 + b, 0:nt * D].rearrange("p (t d) -> p t d", d=D),
                                            rstd[0:KROWS, t0:t0 + nt].unsqueeze(2).to_broadcast([KROWS, nt, D]),
                                            ALU.mult).then_inc(nat_read, 1)
                for c in range(NC if k < NORMS - 1 else 0):
                    close(c)

            def projected(c):
                dve.wait_ge(y_ready, c + 1)
                return ps[:, 6 + c % 2, 0:CW[c]] if c < 2 else ps[:, 0, 0:CW[c]]

            dve.wait_ge(y_ready, 1)
            dve.wait_ge(xt_loaded, 16)
            nc.vector.memset(out_sb[:, N:NPAD], 0.0)
            nc.vector.memset(cen[:, N:NPAD], 0.0)
            nc.vector.memset(sq[:, N:NPAD], 0.0)
            norm(0, projected)
            dense = 0
            lk = 0
            for k, (src, layers, fn) in enumerate(PROPS):
                for st, c in wave(len(layers)):
                    if st == 0:
                        continue
                    dense += 1
                    if fn == "leaky":
                        cs = slice(C0[c], C0[c] + CW[c])
                        dst = out_sb if st == len(layers) else mid[st - 1]
                        dve.wait_ge(act_done, dense)
                        nc.vector.scalar_tensor_tensor(out=dst[:, cs], in0=leak[:, cs], scalar=0.01, in1=leak[:, cs],
                                                       op0=ALU.mult, op1=ALU.max).then_inc(leaky_done, 1)
                        lk += 1
                if k in NORM_AFTER:
                    if fn == "leaky":
                        dve.wait_ge(leaky_done, lk)
                    dve.wait_ge(act_done, dense)
                    norm(NORM_AFTER[k], lambda c: out_sb[:, C0[c]:C0[c] + CW[c]])

        @block.tensor
        def _(pe):
            def score_pair(it, z, p):
                gbase, w = divmod(z, STEPS)
                par = gbase % 2
                sl = slot_of(z) + p
                if not (isinstance(it, int) and it == 0 and sl < 2):
                    pe.wait_ge(s_read, it * (2 * SLOTS) + (sl - 1))
                if PAIR_FROM[w] + p == 0:
                    pe.wait_ge(qk_loaded[par], it * 192 + 192 * (gbase // 2 + 1))
                for e in range(2):
                    i, rest = divmod(2 * (PAIR_FROM[w] + p) + e, HG * NC)
                    a, c = divmod(rest, NC)
                    last = nc.tensor.matmul(ps[:, 2 * (sl % 2) + e, 0:MW], q_sb[0:ZROWS, par, a, P * i:P * i + P],
                                            k_sb[0:ZROWS, par, a, M0[c]:M0[c] + MW], start=True, stop=True)
                last.then_inc(s_ready, 1)

            pe.wait_ge(s_ident, 2)
            for b in range(9):
                if b == 0:
                    pe.wait_ge(x_loaded, 32)
                elif b % 2 == 1 and b >= 3:
                    pe.wait_ge(w_loaded[(b - 3) // 2], 16)
                if b >= 8:
                    pe.wait_ge(wt_read, b - 7)
                for q in range(4):
                    if b >= 3:
                        src = w_nat[:, (b - 3) // 2, 4 * ((b - 3) % 2) + q, :]
                    elif 4 * b + q < T:
                        src = x_nat[0:RP[4 * b + q], 4 * b + q, :]
                    else:
                        continue
                    r = src.shape[0]
                    last = nc.tensor.transpose(ps[:, b % 8, P * q:P * q + r], src, ident[0:r, 0:r])
                last.then_inc(wt_ready, 1)
            pe.wait_ge(wt_read, 9)
            for i in range(T):
                for w in range(3):
                    s = 3 * i + w
                    for h in range(2):
                        if s:
                            pe.wait_ge(proj_read, 2 * s + h - 1)
                        nc.tensor.matmul(ps[0:RP[i], PROJ_BANK + h, :], xT0[:, P * i:P * i + RP[i]],
                                         wT[:, w, 512 * h:512 * h + 512], start=True, stop=True).then_inc(proj_ready, 1)
                pe.wait_ge(adj_loaded[i % 2], 16 * (i // 2 + 1))
                if i == 0:
                    pe.wait_ge(fill, 3)
                cols = adj_nat[i % 2][0:RP[i], 0:T * KROWS].rearrange("p (m t) -> p t m", t=T)
                for b, (t0, nt) in enumerate(TB):
                    n = N_ADJ * i + b
                    if n >= 2:
                        pe.wait_ge(adjt_read, n - 1)
                    for t in range(t0, t0 + nt):
                        last = nc.tensor.transpose(ps[0:KROWS, ADJ_BANK + n % 2, P * (t - t0):P * (t - t0) + RP[i]], cols[:, t, :],
                                                   ident[0:RP[i], 0:RP[i]])
                    last.then_inc(adjt_ready, 1)
                for z in early_steps(i):
                    for p in range(PASS_PAIRS[z]):
                        score_pair(0, z, p)
            pe.wait_ge(bmax_ready, T)
            pe.wait_ge(adjt_read, N_ADJ * T)
            nc.tensor.transpose(ps[:, 7, 0:P], negmax[:], ident[:]).then_inc(brow_ready, 1)
            def turn_max(it, z, sl):
                pe.wait_ge(s_read, it * (2 * SLOTS) + (sl - 1))
                pe.wait_ge(negmax_ready, it * (2 * len(BATCHES)) + (batch_before(z) + 1))
                nc.tensor.transpose(ps[:, 2 * (sl % 2), 0:P], negmax[:], ident[:]).then_inc(s_ready, 1)

            def scores(it, u, a):
                s = u % STEPS
                par = u // STEPS % 2
                c, t = divmod(s, T)
                rows = MAXROWS if kind(u) == MUL else ALLROWS
                if t == 0 and a == 0:
                    pe.wait_ge(maxrow_loaded[c], it * 32 + (16 * (u // STEPS + 1) + 16))
                j = HG * u + a
                jb = j - 3
                if jb >= 0 or not isinstance(it, int) or it > 0:
                    ub = jb // HG
                    if kind(ub) != ADD:
                        pe.wait_ge(exps_done, it * (2 * HG * MULS) + (HG * muls_before(ub) + jb % HG + 1))
                    else:
                        pe.wait_ge(adds_done, it * (2 * HG * ADDS) + (HG * adds_before(ub) + jb % HG + 1))
                bank = ps[0:NKEYS[t], ST_BANK + j % 3, 0:CW[c]]
                nc.tensor.matmul(bank, k_sb[0:rows, par, a, t:t + T * (NKEYS[t] - 1) + 1:T],
                                 q_sb[0:rows, par, a, C0[c]:C0[c] + CW[c]], start=True, stop=True).then_inc(st_ready, 1)

            def values(it, u):
                s = u % STEPS
                par = u // STEPS % 2
                c, t = divmod(s, T)
                if kind(u) == MUL:
                    pe.wait_ge(mults_done, it * (2 * MULS) + (muls_before(u) + 1))
                else:
                    pe.wait_ge(sbexp_done, it * (2 * ADDS) + (adds_before(u) + 1))
                if s == 0:
                    pe.wait_ge(v_loaded[par], it * 32 + 32)
                if t == 0:
                    pe.wait_ge(o_copied, it * (2 * NC) + (u // T + 1))
                r = NKEYS[t]
                for a in range(HG):
                    last = nc.tensor.matmul(ps[32 * a:32 * a + V1, PV_BANK, 0:CW[c]], v_sb[0:r, par, a, V1 * t:V1 * t + V1],
                                            ring[0:r, slot(u), a, 0:CW[c]], start=(t == 0), stop=(t == T - 1))
                last.then_inc(pv_done, 1)

            def step(it, u, maxing, scoring, with_values):
                z = u + AHEAD
                for x in plan(u, maxing):
                    if not isinstance(x, str):
                        score_pair(it, z, x - 10)
                    elif x == "V":
                        if with_values:
                            values(it, u - LAG)
                    elif scoring:
                        scores(it, u, int(x))
                if batch_before(z) is not None and (maxing or z == 2 * STEPS):
                    turn_max(it, z, slot_of(z) + (PASS_PAIRS[z % STEPS] if maxing else 0))

            pe.wait_ge(proj_read, 6 * T)
            for u in range(EARLY[1] - AHEAD, 0):
                step(0, u, True, False, False)
            pe.wait_ge(brow_copied, 16 * PARTS)
            pe.wait_ge(adjt_read, N_ADJ * T)
            for c in range(NC):
                nc.tensor.matmul(ps[0:KROWS, ST_BANK + c, 0:CW[c]], ones3[:], biasrow[:, C0[c]:C0[c] + CW[c]], start=True,
                                 stop=True).then_inc(bb_ready, 1)
            pe.wait_ge(eb_sum, MULS)
            for u in range(LAG):
                step(0, u, True, True, False)
            with pe.Fori(0, NG // 2 - 1) as it:
                for xx in range(2 * STEPS):
                    step(it, xx + LAG, True, True, True)
            for u in range(LAG, 2 * STEPS + LAG):
                step(NG // 2 - 1, u, u + AHEAD < 2 * STEPS, u < 2 * STEPS, True)

            pe.wait_ge(o_copied, NC * NG + 1)

            def project(c):
                pe.wait_ge(ot_read, 2 * min(T, -(-(C0[c] + CW[c]) // P)))
                pe.wait_ge(wot_read, 2)
                dst = ps[:, 6 + c % 2, 0:CW[c]] if c < 2 else ps[:, 0, 0:CW[c]]
                for h in range(H):
                    last = nc.tensor.matmul(dst, woT[:, h, :], oT[:, h, C0[c]:C0[c] + CW[c]], start=(h == 0), stop=(h == H - 1))
                last.then_inc(y_ready, 1)

            for i in range(T):
                if i == 3:
                    pe.wait_ge(wo_loaded, 16)
                    for b in range(2):
                        for h in range(4):
                            last = nc.tensor.transpose(ps[:, 6 + b, P * h:P * h + P],
                                                       wo_nat.rearrange("p (j h) -> p h j", h=H)[:, 4 * b + h, :], ident[:])
                        last.then_inc(wot_ready, 1)
                pe.wait_ge(on_ready, i + 1)
                for b in range(2):
                    n = 2 * i + b
                    if n >= 6:
                        pe.wait_ge(ot_read, n - 5)
                    for h in range(4):
                        last = nc.tensor.transpose(ps[:, n % 6, P * h:P * h + RP[i]], o_nat[i % 3][0:RP[i], 4 * b + h, :],
                                                   ident[0:RP[i], 0:RP[i]])
                    last.then_inc(ot_ready, 1)
                if i in (4, 8):
                    project(i // 4 - 1)
            project(NC - 1)

            def norm(k):
                pe.wait_ge(z_ready, NC * k + NC)
                for c in range(NC):
                    if c == 2:
                        pe.wait_ge(cen_ready, NC * k + 1)
                    nc.tensor.matmul(ps[:, 5 + c % 2, 0:CW[c]], avg[:], z_sb[:, C0[c]:C0[c] + CW[c]], start=True, stop=True).then_inc(mean_ready, 1)
                pe.wait_ge(cen_ready, NC * k + NC)
                naturals(FROM_NORM[k], cen)
                pe.wait_ge(sq_ready, NC * k + NC)
                for t in range(T):
                    last = nc.tensor.matmul(ps[0:KROWS, 2, t:t + 1], sq[:, t:t + T * (KROWS - 1) + 1:T], avg[:, 0:1],
                                            start=True, stop=True)
                last.then_inc(nodevar_ready, 1)
                for c in range(NC if k < NORMS - 1 else 0):
                    nc.tensor.matmul(ps[:, VAR_BANK[c], 0:CW[c]], avg[:], sq[:, C0[c]:C0[c] + CW[c]], start=True,
                                     stop=True).then_inc(var_ready, 1)

            def naturals(k, src):
                cols = src[:, 0:T * KROWS].rearrange("p (m t) -> p t m", t=T)
                for b, (t0, nt) in enumerate(TB):
                    for t in range(t0, t0 + nt):
                        last = nc.tensor.transpose(ps[0:KROWS, 5 + b, P * (t - t0):P * (t - t0) + D], cols[:, t, :], ident[:])
                    last.then_inc(nat_ready, 1)

            pe.wait_ge(small_loaded, 256)
            norm(0)
            dense = 0
            for k, (src, layers, fn) in enumerate(PROPS):
                if src != "x":
                    if fn == "leaky":
                        pe.wait_ge(leaky_done, lk_before(dense))
                    else:
                        pe.wait_ge(act_done, dense)
                    naturals(k, out_sb)
                for st, c in wave(len(layers)):
                    cs = slice(C0[c], C0[c] + CW[c])
                    if st == 0:
                        if k and c == 0:
                            pe.wait_ge(agg_read, NC * k)
                        if src == "x" and c == 1:
                            pe.wait_ge(std_ready, NC * FROM_NORM.index(k) + NC)
                        for t in range(T):
                            if c == 0 and t in (0, 4, 8):
                                pe.wait_ge(nat_read, NC * k + t // 4 + 1)
                            last = nc.tensor.matmul(ps[:, c, 0:CW[c]], nat[0:KROWS, t, :], adjT[0:KROWS, t, cs],
                                                    start=(t == 0), stop=(t == T - 1))
                        last.then_inc(agg_ready, 1)
                        continue
                    if st == 1:
                        pe.wait_ge(agg_read, NC * k + c + 1)
                        rhs = z_sb
                    else:
                        pe.wait_ge(leaky_done, lk_before(dense_index(k, st - 1, c)) + 1)
                        rhs = mid[st - 2]
                    if dense >= 2:
                        pe.wait_ge(act_done, dense - 1)
                    nc.tensor.matmul(ps[:, 3 + dense % 2, 0:CW[c]], wts[:, layers[st - 1], :], rhs[:, cs], start=True,
                                     stop=True).then_inc(dense_ready, 1)
                    dense += 1
                if k in NORM_AFTER:
                    norm(NORM_AFTER[k])


def dense_index(k, st, c):
    before = sum(NC * len(layers) for _, layers, _ in PROPS[:k])
    order = [x for x in wave(len(PROPS[k][1])) if x[0]]
    return before + order.index((st, c))


def lk_before(dense):
    n = 0
    total = 0
    for _, layers, fn in PROPS:
        size = NC * len(layers)
        take = min(size, max(0, dense - total))
        if fn == "leaky":
            n += take
        total += size
    return n


_WEIGHTS = ["L1_gnn_W", "L2_gnn_kernel"] + [f"L3_gnn_{d}_W{i}" for d in ("uv", "vu") for i in (1, 2, 3)]
_BIASES = ["L1_gnn_b", "L2_gnn_bias"] + [f"L3_gnn_{d}_b{i}" for d in ("uv", "vu") for i in (1, 2, 3)]


def kernel(**inputs):
    import numpy as np
    import concourse.bacc as bacc
    from concourse.bass_utils import run_bass_kernel_spmd

    nc = bacc.Bacc("TRN2", target_bir_lowering=False, num_devices=1)
    arrays = {}

    def arg(name):
        a = np.ascontiguousarray(inputs[name])
        arrays["in_" + name] = a
        return nc.dram_tensor("in_" + name, a.shape, mybir.dt.from_np(a.dtype), kind="ExternalInput").ap()

    x, adj = arg("x"), arg("adj")
    wqkv = [arg("L0_gnn_W" + n) for n in "qkv"]
    wo = arg("L0_gnn_Wo")
    weights = [arg(n) for n in _WEIGHTS]
    biases = [arg(n) for n in _BIASES]
    out = nc.dram_tensor("out", (N, D), F32, kind="ExternalOutput").ap()
    build(nc, x, adj, wqkv, wo, weights, biases, out)
    r = run_bass_kernel_spmd(nc, [arrays], core_ids=[0])
    return r.results[0]["out"]
```
